# Optimizing a Trainium2 kernel written in Bass

```python
import numpy as np
import jax
import jax.numpy as jnp

def _softmax(x, axis=-1):
    return jax.nn.softmax(x, axis=axis)
def _gelu(x):
    return jax.nn.gelu(x, approximate=True)
def _silu(x):
    return jax.nn.silu(x)
def _sigmoid(x):
    return jax.nn.sigmoid(x)
def _layernorm(x, axis=-1, eps=1e-5):
    m = jnp.mean(x, axis=axis, keepdims=True)
    v = jnp.var(x, axis=axis, keepdims=True)
    return (x - m) / jnp.sqrt(v + eps)
def _scatter_add(tgt, idx, src, axis=0):
    return tgt.at[idx].add(src)
def _segment_sum(src, seg, n):
    return jax.ops.segment_sum(src, seg, n)

kernel_name = 'mk_conv_seq_d1_conv_nchw256_fca91c'

def setup_inputs(seed: int = 0):
    np.random.seed(seed)
    _w = jnp.asarray
    def _rec_inputs():
        import jax
        import jax.numpy as jnp
        _gk = jax.random.key(seed)
        x = -0.0002091 + 1 * jax.random.normal(jax.random.fold_in(_gk, 1), (32, 256, 56, 56), jnp.float32)
        return x
    x = _rec_inputs()
    def _L0_conv_setup():
        import jax, jax.numpy as jnp
        import numpy as np
        N, C, H, W = (32, 256, 56, 56)
        COUT = 256
        E = 4
        D = 64
        EPS = 1e-05

        def _batchnorm(x, scale, bias):
            m = jnp.mean(x, axis=(0, 2, 3), keepdims=True)
            v = jnp.var(x, axis=(0, 2, 3), keepdims=True)
            xn = (x - m) * jax.lax.rsqrt(v + EPS)
            return xn * scale[None, :, None, None] + bias[None, :, None, None]
        key = jax.random.key(seed)
        ks = jax.random.split(key, 8)
        x = jax.random.normal(ks[0], (N, C, H, W), dtype=jnp.float32)
        dw_w = jax.random.normal(ks[1], (C, 1, 3, 3), dtype=jnp.float32) * 0.1
        bn1_scale = jnp.ones((C,), jnp.float32)
        bn1_bias = jnp.zeros((C,), jnp.float32)
        proj_w = jax.random.normal(ks[2], (D, C), dtype=jnp.float32) * 0.05
        proj_b = jnp.zeros((D,), jnp.float32)
        prototypes = jax.random.normal(ks[3], (E, D), dtype=jnp.float32) * 0.02
        gamma = jnp.array(1.0, jnp.float32)
        expert_w = jax.random.normal(ks[4], (E, COUT, C), dtype=jnp.float32) * 0.05
        bn2_scale = jnp.ones((COUT,), jnp.float32)
        bn2_bias = jnp.zeros((COUT,), jnp.float32)
        return {'x': x, 'dw_w': dw_w, 'bn1_scale': bn1_scale, 'bn1_bias': bn1_bias, 'proj_w': proj_w, 'proj_b': proj_b, 'prototypes': prototypes, 'gamma': gamma, 'expert_w': expert_w, 'bn2_scale': bn2_scale, 'bn2_bias': bn2_bias}
    _L0_conv_all = _L0_conv_setup()
    _L0_conv_in = {k: v for k, v in _L0_conv_all.items() if k in ('dw_w', 'bn1_scale', 'bn1_bias', 'proj_w', 'proj_b', 'prototypes', 'gamma', 'expert_w', 'bn2_scale', 'bn2_bias', )}
    del _L0_conv_all

    return {
        "x": x,
        "L0_conv_dw_w": _L0_conv_in["dw_w"],
        "L0_conv_bn1_scale": _L0_conv_in["bn1_scale"],
        "L0_conv_bn1_bias": _L0_conv_in["bn1_bias"],
        "L0_conv_proj_w": _L0_conv_in["proj_w"],
        "L0_conv_proj_b": _L0_conv_in["proj_b"],
        "L0_conv_prototypes": _L0_conv_in["prototypes"],
        "L0_conv_gamma": _L0_conv_in["gamma"],
        "L0_conv_expert_w": _L0_conv_in["expert_w"],
        "L0_conv_bn2_scale": _L0_conv_in["bn2_scale"],
        "L0_conv_bn2_bias": _L0_conv_in["bn2_bias"],
    }

def reference(x, L0_conv_dw_w, L0_conv_bn1_scale, L0_conv_bn1_bias, L0_conv_proj_w, L0_conv_proj_b, L0_conv_prototypes, L0_conv_gamma, L0_conv_expert_w, L0_conv_bn2_scale, L0_conv_bn2_bias):
    import jax
    import jax.numpy as jnp
    def _L0_conv_ref(x, dw_w, bn1_scale, bn1_bias, proj_w, proj_b, prototypes, gamma, expert_w, bn2_scale, bn2_bias):
        import jax, jax.numpy as jnp
        import numpy as np
        N, C, H, W = (32, 256, 56, 56)
        COUT = 256
        E = 4
        D = 64
        EPS = 1e-05

        def _batchnorm(x, scale, bias):
            m = jnp.mean(x, axis=(0, 2, 3), keepdims=True)
            v = jnp.var(x, axis=(0, 2, 3), keepdims=True)
            xn = (x - m) * jax.lax.rsqrt(v + EPS)
            return xn * scale[None, :, None, None] + bias[None, :, None, None]
        residual = x
        y = jax.lax.conv_general_dilated(x, dw_w, window_strides=(1, 1), padding=((1, 1), (1, 1)), feature_group_count=C, dimension_numbers=('NCHW', 'OIHW', 'NCHW'))
        y = jax.nn.relu(_batchnorm(y, bn1_scale, bn1_bias))
        q = jnp.einsum('nchw,dc->ndhw', y, proj_w) + proj_b[None, :, None, None]
        q_norm2 = jnp.sum(q * q, axis=1)
        p_norm2 = jnp.sum(prototypes * prototypes, axis=1)
        qp = jnp.einsum('ndhw,ed->nehw', q, prototypes)
        dist2 = q_norm2[:, None] + p_norm2[None, :, None, None] - 2.0 * qp
        weights = jax.nn.softmax(-jnp.abs(gamma) * dist2, axis=1)
        expert_out = jnp.einsum('nchw,eoc->neohw', y, expert_w)
        mixed = jnp.einsum('neohw,nehw->nohw', expert_out, weights)
        out = jax.nn.relu(_batchnorm(mixed, bn2_scale, bn2_bias) + residual)
        return out

    def _gn(v, G=32, eps=1e-5):
        B_, C_, H_, W_ = v.shape
        g = v.reshape(B_, G, C_ // G, H_, W_)
        m = jnp.mean(g, axis=(2, 3, 4), keepdims=True)
        s = jnp.var(g, axis=(2, 3, 4), keepdims=True)
        return ((g - m) / jnp.sqrt(s + eps)).reshape(v.shape)

    def _ln_c(v, eps=1e-6):
        m = jnp.mean(v, axis=1, keepdims=True)
        s = jnp.var(v, axis=1, keepdims=True)
        return (v - m) / jnp.sqrt(s + eps)

    def _ln_t(v, eps=1e-5):
        m = jnp.mean(v, axis=-1, keepdims=True)
        s = jnp.var(v, axis=-1, keepdims=True)
        return (v - m) / jnp.sqrt(s + eps)

    def _to_tokens(v):
        B_, C_, H_, W_ = v.shape
        return v.reshape(B_, C_, H_ * W_).transpose(0, 2, 1)
    def _from_tokens(t, like):
        B_, C_, H_, W_ = like.shape
        return t.transpose(0, 2, 1).reshape(B_, C_, H_, W_)

    x = _L0_conv_ref(x, L0_conv_dw_w, L0_conv_bn1_scale, L0_conv_bn1_bias, L0_conv_proj_w, L0_conv_proj_b, L0_conv_prototypes, L0_conv_gamma, L0_conv_expert_w, L0_conv_bn2_scale, L0_conv_bn2_bias)
    return x


_drawn_inputs = setup_inputs


def setup_inputs(seed=0):
    import zlib

    import numpy as np

    out = dict(_drawn_inputs(seed))
    spreads = {'L0_conv_bn1_scale': (1.0, 0.2),
     'L0_conv_bn1_bias': (0.0, 0.1),
     'L0_conv_proj_b': (0.0, 0.676),
     'L0_conv_bn2_scale': (1.0, 0.2),
     'L0_conv_bn2_bias': (0.0, 0.1)}
    factors = {}
    for name, (base, spread) in spreads.items():
        noise = np.random.default_rng([zlib.crc32(name.encode()), seed]).standard_normal(out[name].shape)
        drawn = base * np.exp(spread * noise) if base else spread * noise
        out[name] = jnp.asarray(drawn.astype(out[name].dtype))
    for name, factor in factors.items():
        out[name] = (out[name] * factor).astype(out[name].dtype)
    return out
```

```python
from contextlib import ExitStack

import concourse.bass as bass
from concourse import mybir

fp32 = mybir.dt.float32
f32r = mybir.dt.float32r
ALU = mybir.AluOpType
ACT = mybir.ActivationFunctionType
AX = mybir.AxisListType

N, C, H, W = 32, 256, 56, 56
E, D, COUT = 4, 64, 256
EPS = 1e-5
P = 128
G = C // P
HW = H * W
PIX = N * HW

UNITS = N * G
RING = 4
ROWS = 8
PARTS = H // ROWS
PE_TAPS = [(0, 0), (-1, 0), (1, 0), (0, -1)]
DVE_TAPS = [(dy, dx) for dy in (-1, 0, 1) for dx in (-1, 0, 1) if (dy, dx) not in PE_TAPS]

TILES = 4
CH = TILES * P
CHUNKS = PIX // CH
SLOTS = 4
BANK = 512


def tap(dy, dx):
    return 3 * (dy + 1) + dx + 1


def span(d, n):
    return max(0, -d), min(n, n - d)


def wait(engine, sem, value):
    if isinstance(value, int) and value <= 0:
        return
    engine.wait_ge(sem, value)


def exists(unit):
    return not isinstance(unit, int) or unit >= 0


def build(nc, x, dw, bn1s, bn1b, projT, projb, proto, protoT, gamma, expT, bn2s, bn2b, out):
    conv = nc.dram_tensor("conv_scratch", (G, P, PIX), fp32, kind="Internal").ap()
    mixd = nc.dram_tensor("mixed_scratch", (G, P, PIX), fp32, kind="Internal").ap()
    x_units = x.rearrange("n (g p) h w -> (n g) p (h w)", g=G)
    out_units = out.rearrange("n (g p) h w -> (n g) p (h w)", g=G)
    conv_units = conv.rearrange("g p (n q) -> n g p q", n=N)
    mix_units = mixd.rearrange("g p (n q) -> n g p q", n=N)
    conv_chunks = conv.rearrange("g p (c q) -> c p g q", q=CH)
    mix_chunks = mixd.rearrange("g p (c q) -> c p g q", q=CH)

    ctx = ExitStack()
    with ctx:
        def sb(name, shape, dt=fp32):
            return ctx.enter_context(nc.sbuf_tensor(name, shape, dt))

        def sem(name):
            return ctx.enter_context(nc.semaphore(name))

        xb = sb("x_ring", [P, RING, HW])
        yb = sb("conv_ring", [P, RING, HW])
        ring = xb[:, :, :].rearrange("p r q -> p (r q)")
        cv = ring[:, 0:SLOTS * G * CH].rearrange("p (s g q) -> p s g q", s=SLOTS, g=G)
        mo = ring[:, SLOTS * G * CH:2 * SLOTS * G * CH].rearrange("p (s g q) -> p s g q", s=SLOTS, g=G)
        y32 = sb("y_full", [P, 2, G, CH])
        yh = sb("y_high", [P, SLOTS, G, CH], f32r)
        yl = sb("y_low", [P, SLOTS, G, CH], f32r)
        wload = yb[:, 0, 0:G * E * COUT].rearrange("p (k n) -> p k n", k=G)
        pload = yb[:, 1, 0:G * 2 * D].rearrange("p (k n) -> p k n", k=G)
        wh = sb("experts_high", [P, G, E * COUT], f32r)
        wl = sb("experts_low", [P, G, E * COUT], f32r)
        ph = sb("proj_high", [P, G, 2 * D], f32r)
        pl = sb("proj_low", [P, G, 2 * D], f32r)
        qq = sb("q_and_square", [P, 2, CH])
        to_dist = sb("to_dist", [P, 32])
        logit_rows = sb("logit_rows", [P, 2, P])
        logit_t = sb("logit_pixels", [P, TILES, 32])
        top = sb("top_logit", [P, TILES])
        centered = sb("centered", [P, 2, TILES, E])
        ex = sb("exps", [P, 2, TILES, E])
        total = sb("exp_sum", [P, TILES])
        inv_total = sb("exp_sum_inverse", [P, TILES])
        gate = sb("gates", [P, 2, TILES, E])
        mix = sb("mix_ring", [P, TILES, COUT])
        ident = sb("identity", [P, P])
        diag = sb("tap_diagonals", [P, G, len(PE_TAPS), P])
        taps = sb("taps", [P, G, 9])
        st1 = sb("stats1_now", [P, RING, PARTS, 6])
        st1_all = sb("stats1", [P, UNITS // RING, RING, PARTS * 6])
        st2 = sb("stats2_now", [P, SLOTS, G, 6])
        st2_all = sb("stats2", [P, CHUNKS // SLOTS, SLOTS, G, 6])
        bnp = sb("bn_params", [P, 4, G])
        mv = sb("mean_var", [P, G, 2])
        var_eps, root_of = sb("var_eps", [P, G]), sb("root_of_var", [P, G])
        inverse, newton = sb("inverse_root", [P, G]), sb("newton", [P, G])
        aff = sb("bn_affine", [P, 2, 2, G])
        qb = sb("proj_bias", [P, 1])
        gam = sb("gamma_signs", [P, 3])
        pro = sb("prototypes", [P, D])
        prosq = sb("prototypes_sq", [P, D])
        pn2 = sb("prototype_norms", [P, 2])

        banks = [ctx.enter_context(nc.psum_tensor(f"bank{i}", [P, BANK], fp32)) for i in range(8)]
        expert_ps = [(banks[0], banks[1]), (banks[2], banks[3])]
        q_ps = banks[4]
        tr_ps = [banks[5], banks[6]]

        params = sem("params_loaded")
        ident_cleared, ident_ready = sem("ident_cleared"), sem("ident_ready")
        cleared, norms_ready, weights_ready = sem("cleared"), sem("norms_ready"), sem("weights_ready")
        x_in = [sem(f"x_loaded{i}") for i in range(RING)]
        setup, norm_step = sem("setup_steps"), sem("norm_steps")
        tap_added, stats1_kept, stats2_kept = sem("tap_added"), sem("stats1_kept"), sem("stats2_kept")
        turned, top_ready = sem("logits_turned"), sem("top_ready")
        total_ready, inverse_ready, expert_added = sem("total_ready"), sem("inverse_ready"), sem("expert_added")
        part_done, part_copied = sem("conv_part_done"), sem("conv_part_copied")
        conv_ready, conv_measured = sem("conv_ready"), sem("conv_measured")
        conv_out = [sem(f"conv_stored{i}") for i in range(RING)]
        var_ready, root_ready, norm_ready = sem("var_ready"), sem("root_ready"), sem("norm_ready")
        conv_in = [sem(f"conv_loaded{i}") for i in range(SLOTS)]
        y_full, y_high, y_low = sem("y_full"), sem("y_high"), sem("y_low")
        q_done, qq_ready = sem("q_done"), sem("qq_ready")
        dist_done, logits_ready = sem("dist_done"), sem("logits_ready")
        centered_ready, exp_ready, gates_ready = sem("centered_ready"), sem("exp_ready"), sem("gates_ready")
        experts_done, mix_begun, mixed = sem("experts_done"), sem("mix_begun"), sem("mixed")
        transposed, evacuated, mix_measured = sem("transposed"), sem("evacuated"), sem("mix_measured")
        mix_out = [sem(f"mix_stored{i}") for i in range(SLOTS)]
        x_again = [sem(f"x_reloaded{i}") for i in range(RING)]
        mix_in = [sem(f"mix_reloaded{i}") for i in range(RING)]
        summed, out_ready = sem("residual_added"), sem("out_ready")
        out_stored = [sem(f"out_stored{i}") for i in range(RING)]

        block = ctx.enter_context(nc.Block())
        ITS1, ITS2 = UNITS // RING, CHUNKS // SLOTS
        N_PARAM_DMAS = 16

        def staged(engine, its, body):
            body(0, False)
            body(1, False)
            with engine.Fori(2, its - 1) as it:
                body(it, False)
            body(its - 1, True)

        @block.sync
        def _(sp):
            with nc.allow_non_contiguous_dma(reason="small parameters, once"):
                sp.dma_start(taps[:, :, :], dw.rearrange("(g p) t -> p g t", g=G)).then_inc(params, 16)
                sp.dma_start(gam[:, 0:1], gamma.partition_broadcast(P)).then_inc(params, 16)
                for i, v in enumerate((bn1s, bn1b, bn2s, bn2b)):
                    sp.dma_start(bnp[:, i, :], v.rearrange("(g p) -> p g", g=G)).then_inc(params, 16)
                for h in range(2):
                    sp.dma_start(qb[D * h:D * h + D, :], projb.rearrange("(p a) -> p a", a=1)).then_inc(params, 16)
                    sp.dma_start(pload[:, :, D * h:D * h + D],
                                 projT.rearrange("(k p) d -> p k d", k=G)).then_inc(params, 16)
                sp.dma_start(wload, expT.rearrange("(k p) n -> p k n", k=G)).then_inc(params, 16)
                sp.wait_ge(cleared, 1)
                sp.dma_start(to_dist[0:D, 0:E], protoT).then_inc(params, 16)
                for j in range(4):
                    sp.dma_start(pro[32 * j:32 * j + E, :], proto).then_inc(params, 16)

            def load_unit(n, g, slot):
                sp.dma_start(xb[:, slot, :], x_units[n * G + g]).then_inc(x_in[slot], 16)

            for k in range(RING - 1):
                load_unit(k // G, k % G, k)

            def body1(it, last):
                for k in range(RING):
                    u = RING * it + k
                    ahead = k + RING - 1
                    if not (last and ahead >= RING):
                        wait(sp, conv_ready, u)
                        load_unit(2 * it + ahead // G, ahead % G, ahead % RING)
                    sp.wait_ge(conv_ready, u + 1)
                    sp.dma_start(conv_units[2 * it + k // G, k % G], yb[:, k, :]).then_inc(conv_out[k], 16)
            staged(sp, ITS1, body1)

            for k in range(RING):
                sp.wait_ge(conv_out[k], 16 * ITS1)

            def load_chunk(c, slot):
                sp.dma_start(cv[:, slot], conv_chunks[c]).then_inc(conv_in[slot], 16)

            for c in range(SLOTS - 1):
                load_chunk(c, c)

            def body2(it, last):
                for j in range(SLOTS):
                    c = SLOTS * it + j
                    if not (last and j + SLOTS - 1 >= SLOTS):
                        wait(sp, y_full, c)
                        load_chunk(c + SLOTS - 1, (j + SLOTS - 1) % SLOTS)
                    sp.wait_ge(evacuated, c + 1)
                    sp.dma_start(mix_chunks[c], mo[:, j]).then_inc(mix_out[j], 16)
            staged(sp, ITS2, body2)

            for j in range(SLOTS):
                sp.wait_ge(mix_out[j], 16 * ITS2)
            sp.wait_ge(mix_measured, CHUNKS)

            def load_pair(n, g, slot):
                sp.dma_start(xb[:, slot, :], x_units[n * G + g]).then_inc(x_again[slot], 16)
                sp.dma_start(yb[:, slot, :], mix_units[n, g]).then_inc(mix_in[slot], 16)

            for k in range(RING - 1):
                load_pair(k // G, k % G, k)

            def body3(it, last):
                for k in range(RING):
                    u = RING * it + k
                    ahead = k + RING - 1
                    slot = ahead % RING
                    if not (last and ahead >= RING):
                        wait(sp, out_stored[slot], 16 * (it + ahead // RING))
                        load_pair(2 * it + ahead // G, ahead % G, slot)
                    sp.wait_ge(out_ready, u + 1)
                    sp.dma_start(out_units[u], yb[:, k, :]).then_inc(out_stored[k], 16)
            staged(sp, ITS1, body3)
            for k in range(RING):
                sp.wait_ge(out_stored[k], 16 * ITS1)

        @block.gpsimd
        def _(pool):
            nc.gpsimd.memset(ident[:, :], 0.0).then_inc(ident_cleared, 1)
            pool.wait_ge(ident_cleared, 1)
            nc.gpsimd.affine_select(out=ident[:, :], in_=ident[:, :], compare_op=ALU.not_equal, fill=1.0, base=0,
                                    pattern=[[-1, P]], channel_multiplier=1).then_inc(ident_ready, 1)

            def body2(it, last):
                for j in range(SLOTS):
                    c = SLOTS * it + j
                    pool.wait_ge(y_high, c + 1)
                    nc.gpsimd.tensor_tensor(yl[:, j], y32[:, j % 2], yh[:, j].bitcast(fp32),
                                            ALU.subtract).then_inc(y_low, 1)
            staged(pool, ITS2, body2)

        @block.scalar
        def _(act):
            act.wait_ge(params, 16 * N_PARAM_DMAS)
            nc.scalar.activation(prosq[:, :], pro[:, :], ACT.Square, accum_out=pn2[:, 0:1]).then_inc(norms_ready, 1)

            def body1(it, last):
                for k in range(RING):
                    u = RING * it + k
                    wait(act, conv_out[k], 16 * it)
                    wait(act, conv_measured, u - RING + 1)
                    for r in range(PARTS):
                        act.wait_ge(part_done, PARTS * u + r + 1)
                        nc.scalar.activation(yb[:, k, r * ROWS * W:(r + 1) * ROWS * W], banks[r][:, 0:ROWS * W],
                                             ACT.Copy).then_inc(part_copied, 1)
            act.wait_ge(weights_ready, 1)
            staged(act, ITS1, body1)

            def root(n):
                act.wait_ge(var_ready, n + 1)
                nc.scalar.activation(root_of[:, :], var_eps[:, :], ACT.Sqrt).then_inc(root_ready, 1)
            root(0)
            act.wait_ge(norm_ready, 1)

            def relu(c, it, j):
                act.wait_ge(conv_in[j % SLOTS], 16 * (it + 1 + j // SLOTS))
                wait(act, y_low, c - 1)
                for g in range(G):
                    done = nc.scalar.activation(y32[:, j % 2, g], cv[:, j % SLOTS, g], ACT.Relu,
                                                scale=aff[:, 0, 0, g:g + 1], bias=aff[:, 0, 1, g:g + 1])
                done.then_inc(y_full, 1)

            def square(c, j):
                act.wait_ge(q_done, c + 1)
                wait(act, dist_done, c - 1)
                nc.scalar.activation(qq[0:D, j % 2], q_ps[0:D, :], ACT.Identity, bias=qb[0:D, :])
                nc.scalar.activation(qq[D:P, j % 2], q_ps[D:P, :], ACT.Square, bias=qb[D:P, :]).then_inc(qq_ready, 1)

            def logits(c, j):
                act.wait_ge(dist_done, c + 1)
                wait(act, centered_ready, c - 1)
                nc.scalar.activation(logit_rows[:, j % 2], q_ps[:, 0:P], ACT.Identity,
                                     scale=gam[:, 2:3], bias=pn2[:, 1:2]).then_inc(logits_ready, 1)

            def exps(c, j):
                act.wait_ge(centered_ready, c + 1)
                wait(act, gates_ready, c - 1)
                nc.scalar.activation(ex[:, j % 2], centered[:, j % 2], ACT.Exp).then_inc(exp_ready, 1)

            def begin_mix(c, j, t):
                if t == 0:
                    act.wait_ge(gates_ready, c + 1)
                act.wait_ge(experts_done, TILES * c + t + 1)
                wait(act, transposed, TILES * (c - 1) + t + 1)
                nc.scalar.activation(mix[:, t], expert_ps[t % 2][0][:, 0:COUT], ACT.Copy,
                                     scale=gate[:, j % 2, t, 0:1]).then_inc(mix_begun, 1)

            def evacuate(c, it, j):
                act.wait_ge(transposed, TILES * (c + 1))
                wait(act, mix_out[j], 16 * it)
                wait(act, mix_measured, c - SLOTS + 1)
                for g in range(G):
                    done = nc.scalar.activation(mo[:, j, g], tr_ps[g][:, :], ACT.Copy)
                done.then_inc(evacuated, 1)

            relu(0, 0, 0)
            relu(1, 0, 1)
            square(0, 0)
            logits(0, 0)
            exps(0, 0)

            def body2(it, last):
                for j in range(SLOTS):
                    c = SLOTS * it + j
                    begin_mix(c, j, 0)
                    if exists(c - 1):
                        evacuate(c - 1, it if j else it - 1, (j - 1) % SLOTS)
                    if not (last and j + 2 >= SLOTS):
                        relu(c + 2, it, j + 2)
                    more = not (last and j + 1 >= SLOTS)
                    if more:
                        square(c + 1, j + 1)
                    begin_mix(c, j, 1)
                    if more:
                        logits(c + 1, j + 1)
                    begin_mix(c, j, 2)
                    if more:
                        exps(c + 1, j + 1)
                    begin_mix(c, j, 3)
            staged(act, ITS2, body2)
            evacuate(CHUNKS - 1, ITS2 - 1, SLOTS - 1)
            root(1)

            def body3(it, last):
                for k in range(RING):
                    act.wait_ge(summed, RING * it + k + 1)
                    nc.scalar.activation(yb[:, k, :], yb[:, k, :], ACT.Relu,
                                         bias=aff[:, 1, 1, k % G:k % G + 1]).then_inc(out_ready, 1)
            staged(act, ITS1, body3)

        @block.tensor
        def _(pe):
            pe.wait_ge(weights_ready, 1)

            def body1(it, last):
                for k in range(RING):
                    u = RING * it + k
                    pe.wait_ge(x_in[k], 16 * (it + 1))
                    image = xb[:, k, :].rearrange("p (h w) -> p h w", w=W)
                    for r in range(PARTS):
                        wait(pe, part_copied, PARTS * (u - 1) + r + 1)
                        sums = banks[r][:, 0:ROWS * W].rearrange("p (h w) -> p h w", w=W)
                        for i, (dy, dx) in enumerate(PE_TAPS):
                            (h0, h1), (w0, w1) = span(dy, H), span(dx, W)
                            h0, h1 = max(h0, r * ROWS), min(h1, (r + 1) * ROWS)
                            done = nc.tensor.matmul(sums[:, h0 - r * ROWS:h1 - r * ROWS, w0:w1],
                                                    diag[:, k % G, i, :],
                                                    image[:, h0 + dy:h1 + dy, w0 + dx:w1 + dx],
                                                    start=i == 0, stop=i == len(PE_TAPS) - 1)
                        done.then_inc(part_done, 1)
            staged(pe, ITS1, body1)

            def project(c, j):
                pe.wait_ge(y_low, c + 1)
                wait(pe, logits_ready, c)
                passes = [(w, y, k) for k in range(G) for w, y in ((ph, yh), (pl, yh), (ph, yl))]
                for i, (w, y, k) in enumerate(passes):
                    done = nc.tensor.matmul(q_ps[:, :], w[:, k, :], y[:, j % SLOTS, k, :],
                                            start=i == 0, stop=i == len(passes) - 1)
                done.then_inc(q_done, 1)

            def distances(c, j):
                pe.wait_ge(qq_ready, c + 1)
                pixels = qq[:, j % 2, :].rearrange("p (t b q) -> p b t q", t=TILES, q=32)
                for b in range(4):
                    done = nc.tensor.matmul(q_ps[32 * b:32 * b + 32, 0:P], to_dist[:, :], pixels[:, b],
                                            start=True, stop=True)
                done.then_inc(dist_done, 1)

            def experts(c, j, t):
                wait(pe, mixed, TILES * c + t - 1)
                for k in range(G):
                    for y, weights in ((yh, (wh, wl)), (yl, (wh,))):
                        for w in weights:
                            for half in range(2):
                                done = nc.tensor.matmul(
                                    expert_ps[t % 2][half][:, :], y[:, j, k, t * P:(t + 1) * P],
                                    w[:, k, half * BANK:(half + 1) * BANK],
                                    start=k == 0 and y is yh and w is wh, stop=k == G - 1 and y is yl)
                done.then_inc(experts_done, 1)

            def transpose(c, t):
                pe.wait_ge(mixed, TILES * c + t + 1)
                if t == 0:
                    wait(pe, evacuated, c)
                for g in range(G):
                    done = nc.tensor.transpose(tr_ps[g][:, t * P:(t + 1) * P], mix[:, t, g * P:(g + 1) * P],
                                               ident[:, :])
                done.then_inc(transposed, 1)

            pe.wait_ge(norm_ready, 1)
            project(0, 0)
            distances(0, 0)

            def body2(it, last):
                for j in range(SLOTS):
                    c = SLOTS * it + j
                    more = not (last and j + 1 >= SLOTS)
                    experts(c, j, 0)
                    if exists(c - 1):
                        transpose(c - 1, 3)
                    if more:
                        project(c + 1, j + 1)
                    experts(c, j, 1)
                    transpose(c, 0)
                    if more:
                        distances(c + 1, j + 1)
                    experts(c, j, 2)
                    transpose(c, 1)
                    experts(c, j, 3)
                    transpose(c, 2)
            staged(pe, ITS2, body2)
            transpose(CHUNKS - 1, 3)

        @block.vector
        def _(dve):
            steps = [0]

            def then(instruction):
                instruction.then_inc(setup, 1)
                steps[0] += 1
                dve.wait_ge(setup, steps[0])

            nc.vector.memset(pro[:, :], 0.0)
            then(nc.vector.memset(to_dist[:, :], 0.0))
            nc.vector.memset(to_dist[D:P, 0:E], 1.0).then_inc(cleared, 1)
            dve.wait_ge(params, 16 * N_PARAM_DMAS)
            dve.wait_ge(ident_ready, 1)
            for whole, high, low in ((wload, wh, wl), (pload, ph, pl)):
                then(nc.vector.tensor_copy(high[:, :, :], whole))
                nc.vector.tensor_tensor(low[:, :, :], whole, high[:, :, :].bitcast(fp32), ALU.subtract)
            nc.vector.tensor_scalar(to_dist[0:D, 0:E], to_dist[0:D, 0:E], -2.0, None, ALU.mult)
            then(nc.vector.tensor_scalar(gam[:, 1:2], gam[:, 0:1], -1.0, None, ALU.mult))
            then(nc.vector.tensor_tensor(gam[:, 2:3], gam[:, 0:1], gam[:, 1:2], ALU.min))
            dve.wait_ge(norms_ready, 1)
            nc.vector.tensor_tensor(pn2[:, 1:2], pn2[:, 0:1], gam[:, 2:3], ALU.mult)
            for g in range(G):
                for i, (dy, dx) in enumerate(PE_TAPS):
                    done = nc.vector.tensor_scalar(diag[:, g, i, :], ident[:, :],
                                                   taps[:, g, tap(dy, dx):tap(dy, dx) + 1], None, ALU.mult)
            done.then_inc(weights_ready, 1)

            def body1(it, last):
                for k in range(RING):
                    u = RING * it + k
                    dve.wait_ge(part_copied, PARTS * (u + 1))
                    image = xb[:, k, :].rearrange("p (h w) -> p h w", w=W)
                    sums = yb[:, k, :].rearrange("p (h w) -> p h w", w=W)
                    for i, (dy, dx) in enumerate(DVE_TAPS):
                        if i:
                            dve.wait_ge(tap_added, (len(DVE_TAPS) - 1) * u + i)
                        (h0, h1), (w0, w1) = span(dy, H), span(dx, W)
                        onto = sums[:, h0:h1, w0:w1]
                        done = nc.vector.scalar_tensor_tensor(
                            out=onto, in0=image[:, h0 + dy:h1 + dy, w0 + dx:w1 + dx],
                            scalar=taps[:, k % G, tap(dy, dx):tap(dy, dx) + 1], in1=onto,
                            op0=ALU.mult, op1=ALU.add)
                        done.then_inc(tap_added if i < len(DVE_TAPS) - 1 else conv_ready, 1)
                    dve.wait_ge(conv_ready, u + 1)
                    if k == 0:
                        wait(dve, stats1_kept, it)
                    for r in range(PARTS):
                        done = nc.vector.bn_stats(st1[:, k, r, :], yb[:, k, r * ROWS * W:(r + 1) * ROWS * W])
                    done.then_inc(conv_measured, 1)
                dve.wait_ge(conv_measured, RING * (it + 1))
                nc.vector.tensor_copy(st1_all[:, it].rearrange("p k s -> p (k s)"),
                                      st1[:, :, :, :].rearrange("p k r s -> p (k r s)")).then_inc(stats1_kept, 1)
            staged(dve, ITS1, body1)

            norm_steps = [0]

            def step(instruction):
                instruction.then_inc(norm_step, 1)
                norm_steps[0] += 1
                dve.wait_ge(norm_step, norm_steps[0])

            def normalise(n, stats, kept):
                dve.wait_ge(kept, ITS1 if n == 0 else ITS2)
                for g in range(G):
                    step(nc.vector.bn_aggr(mv[:, g, :], stats(g)))
                nc.vector.tensor_scalar(var_eps[:, :], mv[:, :, 1], EPS, None, ALU.add).then_inc(var_ready, 1)
                dve.wait_ge(root_ready, n + 1)
                step(nc.vector.reciprocal(inverse[:, :], root_of[:, :]))
                step(nc.vector.tensor_tensor(newton[:, :], inverse[:, :], inverse[:, :], ALU.mult))
                step(nc.vector.tensor_tensor(newton[:, :], newton[:, :], var_eps[:, :], ALU.mult))
                step(nc.vector.tensor_scalar(newton[:, :], newton[:, :], -0.5, 1.5, ALU.mult, ALU.add))
                step(nc.vector.tensor_tensor(inverse[:, :], inverse[:, :], newton[:, :], ALU.mult))
                step(nc.vector.tensor_tensor(aff[:, n, 0], inverse[:, :], bnp[:, 2 * n], ALU.mult))
                step(nc.vector.tensor_tensor(newton[:, :], mv[:, :, 0], aff[:, n, 0], ALU.mult))
                nc.vector.tensor_tensor(aff[:, n, 1], bnp[:, 2 * n + 1], newton[:, :],
                                        ALU.subtract).then_inc(norm_ready, 1)
            normalise(0, lambda g: st1_all[:, :, :, :].rearrange("p i (n g) s -> p (i n) g s", g=G)[:, :, g],
                      stats1_kept)

            def round_y(c, j):
                dve.wait_ge(y_full, c + 1)
                wait(dve, experts_done, TILES * (c - SLOTS + 1))
                nc.vector.tensor_copy(yh[:, j % SLOTS], y32[:, j % 2]).then_inc(y_high, 1)

            def center(c, j):
                dve.wait_ge(logits_ready, c + 1)
                wait(dve, centered_ready, c)
                nc.vector.transpose(logit_t[:, :, :].rearrange("p t e -> p (t e)"),
                                    logit_rows[:, j % 2]).then_inc(turned, 1)
                dve.wait_ge(turned, c + 1)
                nc.vector.tensor_reduce(out=top[:, :], in_=logit_t[:, :, 0:E], axis=AX.X,
                                        op=ALU.max).then_inc(top_ready, 1)
                dve.wait_ge(top_ready, c + 1)
                nc.vector.tensor_tensor(centered[:, j % 2], logit_t[:, :, 0:E],
                                        top[:, :].unsqueeze(2).broadcast_to([P, TILES, E]),
                                        ALU.subtract).then_inc(centered_ready, 1)

            def gates(c, j):
                dve.wait_ge(exp_ready, c + 1)
                wait(dve, gates_ready, c)
                nc.vector.tensor_reduce(out=total[:, :], in_=ex[:, j % 2], axis=AX.X,
                                        op=ALU.add).then_inc(total_ready, 1)
                dve.wait_ge(total_ready, c + 1)
                nc.vector.reciprocal(inv_total[:, :], total[:, :]).then_inc(inverse_ready, 1)
                dve.wait_ge(inverse_ready, c + 1)
                wait(dve, mixed, TILES * (c - 1))
                nc.vector.tensor_tensor(gate[:, j % 2], ex[:, j % 2],
                                        inv_total[:, :].unsqueeze(2).broadcast_to([P, TILES, E]),
                                        ALU.mult).then_inc(gates_ready, 1)

            def mix_tile(c, j, t):
                dve.wait_ge(mix_begun, TILES * c + t + 1)
                for e in range(1, E):
                    if e > 1:
                        dve.wait_ge(expert_added, (E - 2) * (TILES * c + t) + e - 1)
                    done = nc.vector.scalar_tensor_tensor(
                        out=mix[:, t], in0=expert_ps[t % 2][e // 2][:, (e % 2) * COUT:(e % 2 + 1) * COUT],
                        scalar=gate[:, j % 2, t, e:e + 1], in1=mix[:, t], op0=ALU.mult, op1=ALU.add)
                    done.then_inc(expert_added if e < E - 1 else mixed, 1)

            def measure(c, it, j):
                dve.wait_ge(evacuated, c + 1)
                if j == 0:
                    wait(dve, stats2_kept, it)
                for g in range(G):
                    done = nc.vector.bn_stats(st2[:, j, g, :], mo[:, j, g])
                done.then_inc(mix_measured, 1)

            def keep_stats(it):
                dve.wait_ge(mix_measured, SLOTS * (it + 1))
                nc.vector.tensor_copy(st2_all[:, it].rearrange("p j g s -> p (j g s)"),
                                      st2[:, :, :, :].rearrange("p j g s -> p (j g s)")).then_inc(stats2_kept, 1)

            round_y(0, 0)
            round_y(1, 1)
            center(0, 0)
            gates(0, 0)

            def body2(it, last):
                for j in range(SLOTS):
                    c = SLOTS * it + j
                    more = not (last and j + 1 >= SLOTS)
                    mix_tile(c, j, 0)
                    if not (last and j + 2 >= SLOTS):
                        round_y(c + 2, j + 2)
                    mix_tile(c, j, 1)
                    if exists(c - 1):
                        measure(c - 1, it if j else it - 1, (j - 1) % SLOTS)
                        if j == 0:
                            keep_stats(it - 1)
                    if more:
                        center(c + 1, j + 1)
                    mix_tile(c, j, 2)
                    if more:
                        gates(c + 1, j + 1)
                    mix_tile(c, j, 3)
            staged(dve, ITS2, body2)
            measure(CHUNKS - 1, ITS2 - 1, SLOTS - 1)
            keep_stats(ITS2 - 1)
            normalise(1, lambda g: st2_all[:, :, :, :].rearrange("p i j g s -> p (i j) g s")[:, :, g],
                      stats2_kept)

            def body3(it, last):
                for k in range(RING):
                    dve.wait_ge(x_again[k], 16 * (it + 1))
                    dve.wait_ge(mix_in[k], 16 * (it + 1))
                    nc.vector.scalar_tensor_tensor(out=yb[:, k, :], in0=yb[:, k, :],
                                                   scalar=aff[:, 1, 0, k % G:k % G + 1], in1=xb[:, k, :],
                                                   op0=ALU.mult, op1=ALU.add).then_inc(summed, 1)
            staged(dve, ITS1, body3)


def kernel(**inputs):
    import numpy as np
    import concourse.bacc as bacc
    from concourse.bass_utils import run_bass_kernel_spmd

    arr = {k.replace("L0_conv_", ""): np.asarray(v) for k, v in inputs.items()}
    laid = {
        "x": arr["x"],
        "dw": arr["dw_w"].reshape(C, 9),
        "bn1s": arr["bn1_scale"], "bn1b": arr["bn1_bias"],
        "projT": arr["proj_w"].T, "projb": arr["proj_b"],
        "proto": arr["prototypes"], "protoT": arr["prototypes"].T,
        "gamma": arr["gamma"].reshape(1),
        "expT": arr["expert_w"].transpose(2, 0, 1).reshape(C, E * COUT),
        "bn2s": arr["bn2_scale"], "bn2b": arr["bn2_bias"],
    }
    laid = {k: np.ascontiguousarray(v) for k, v in laid.items()}
    nc = bacc.Bacc("TRN2", target_bir_lowering=False, num_devices=1)
    args = [nc.dram_tensor(f"in_{k}", v.shape, mybir.dt.from_np(v.dtype), kind="ExternalInput").ap() for k, v in laid.items()]
    out = nc.dram_tensor("out", (N, COUT, H, W), fp32, kind="ExternalOutput").ap()
    build(nc, *args, out)
    result = run_bass_kernel_spmd(nc, [{f"in_{k}": v for k, v in laid.items()}], core_ids=[0])
    return result.results[0]["out"]
```

```python
from contextlib import ExitStack

import concourse.bass as bass
from concourse import mybir

fp32 = mybir.dt.float32
f32r = mybir.dt.float32r
ALU = mybir.AluOpType
ACT = mybir.ActivationFunctionType
AX = mybir.AxisListType

N, C, H, W = 32, 256, 56, 56
E, D, COUT = 4, 64, 256
EPS = 1e-5
P = 128
G = C // P
HW = H * W
PIX = N * HW

IMAGES = 2
BLOCKS0 = P // 32
QUARTER = HW // 4
Q_ROWS = H // 4
SUB_ROWS = Q_ROWS // 2
ROWS = 8
PARTS = H // ROWS
TAPS = [(dy, dx) for dy in (-1, 0, 1) for dx in (-1, 0, 1)]
PE_TAPS = [[(0, 0)], [(0, 0), (-1, 0)]]
DVE_TAPS = [[t for t in TAPS if t not in on_pe] for on_pe in PE_TAPS]
MAX_PE_TAPS = max(map(len, PE_TAPS))
HALF = HW // 2

UNITS = N * G
RING = 4

TILES = 4
CH = TILES * P
CHUNKS = PIX // CH
SLOTS = 4
BANK = 512
BLOCKS = COUT // 32


def tap(dy, dx):
    return 3 * (dy + 1) + dx + 1


def span(d, n):
    return max(0, -d), min(n, n - d)


def wait(engine, sem, value):
    if isinstance(value, int) and value <= 0:
        return
    engine.wait_ge(sem, value)


def exists(unit):
    return not isinstance(unit, int) or unit >= 0


def build(nc, x, dw, bn1s, bn1b, projT, projb, proto, protoT, gamma, expT, bn2s, bn2b, out):
    conv = nc.dram_tensor("conv_scratch", (G, P, PIX), fp32, kind="Internal").ap()
    mixd = nc.dram_tensor("mixed_scratch", (G, P, PIX), fp32, kind="Internal").ap()
    x_units = x.rearrange("n (g p) h w -> (n g) p (h w)", g=G)
    out_units = out.rearrange("n (g p) h w -> (n g) p (h w)", g=G)
    conv_images = conv.rearrange("g p (n q) -> g n p q", n=N)
    conv_quarters = conv.rearrange("g (b c) (n a q) -> g n b a c q", c=32, n=N, a=4)
    mix_units = mixd.rearrange("g p (n q) -> n g p q", n=N)
    conv_chunks = conv.rearrange("g p (c q) -> c p g q", q=CH)
    mix_blocks = mixd.rearrange("g (h i) (c a q) -> c a i (g h) q", i=32, a=4, q=P)
    blocks_dram = [nc.dram_tensor(f"block_stats{n}", (P, blocks * 3), fp32, kind="Internal").ap()
                   for n, blocks in enumerate((BLOCKS0, BLOCKS))]

    ctx = ExitStack()
    with ctx:
        def sb(name, shape, dt=fp32):
            return ctx.enter_context(nc.sbuf_tensor(name, shape, dt))

        def sem(name):
            return ctx.enter_context(nc.semaphore(name))

        xb = sb("x_ring", [P, RING, HW])
        yb = sb("conv_ring", [P, RING, HW])
        stack = xb
        conv1, x1 = yb[:, 0:IMAGES], yb[:, IMAGES:2 * IMAGES]
        conv0 = sb("conv_blocks", [P, BLOCKS0, QUARTER])
        stack_w = sb("stack_weights", [P, BLOCKS0, 3, 32])
        stack_taps = sb("stack_taps", [P, BLOCKS0, 3])
        ring = xb[:, :, :].rearrange("p r q -> p (r q)")
        cv = ring[:, 0:SLOTS * G * CH].rearrange("p (s g q) -> p s g q", s=SLOTS, g=G)
        mo = ring[:, SLOTS * G * CH:2 * SLOTS * G * CH].rearrange("p (s b r q) -> p s b r q", s=2, b=BLOCKS, r=2)
        y32 = sb("y_full", [P, 2, G, CH])
        yh = sb("y_high", [P, SLOTS, G, CH], f32r)
        yl = sb("y_low", [P, SLOTS, G, CH], f32r)
        wload = yb[:, 0, 0:G * E * COUT].rearrange("p (k n) -> p k n", k=G)
        pload = yb[:, 1, 0:G * D].rearrange("p (k n) -> p k n", k=G)
        wh = sb("experts_high", [P, G, E * COUT], f32r)
        wl = sb("experts_low", [P, G, E * COUT], f32r)
        proj_for_high = sb("proj_high_low", [P, G, 2 * D], f32r)
        proj_for_low = sb("proj_none_high", [P, G, 2 * D], f32r)
        q_cross = sb("q_cross", [D, CH])
        qq = sb("q_and_square", [P, 2, CH])
        to_dist = sb("to_dist", [P, 32])
        logit_rows = sb("logit_rows", [P, 2, P])
        logit_t = sb("logit_pixels", [P, TILES, 32])
        top = sb("top_logit", [P, TILES])
        centered = sb("centered", [P, 2, TILES, E])
        ex = sb("exps", [P, 2, TILES, E])
        total = sb("exp_sum", [P, TILES])
        inv_total = sb("exp_sum_inverse", [P, TILES])
        gate = sb("gates", [P, 2, TILES, E])
        mix = sb("mix_ring", [P, TILES, COUT])
        ident = sb("identity", [P, P])
        diag = sb("tap_diagonals", [P, MAX_PE_TAPS, P])
        taps = sb("taps", [P, 9])
        halves = sb("half_sums", [P, IMAGES, 2, 2])
        image_sum = sb("image_sum", [P, IMAGES])
        minus_mean = sb("image_minus_mean", [P, IMAGES])
        block_sum = sb("block_sum", [P, IMAGES, BLOCKS0])
        block_minus_mean = sb("block_minus_mean", [P, IMAGES, BLOCKS0])
        block_squares = sb("block_squares", [P, IMAGES, BLOCKS0])
        st0 = sb("stats_group0", [P, N // IMAGES, IMAGES, BLOCKS0, 3])
        st1 = sb("stats_group1", [P, N // IMAGES, IMAGES, 3])
        st2 = sb("stats2_now", [P, 2, BLOCKS, 6])
        body_mv = sb("body_mean_var", [P, BLOCKS, 2])
        st2_all = sb("stats2", [P, CHUNKS // SLOTS, BLOCKS, 3])
        block_mv = sb("block_mean_var", [P, BLOCKS, 2])
        block_st = sb("block_stats_out", [P, BLOCKS, 3])
        channel_st = sb("channel_stats", [P, G, 4, 3])
        bnp = sb("bn_params", [P, 4, G])
        mv = sb("mean_var", [P, G, 2])
        var_eps, root_of = sb("var_eps", [P, G]), sb("root_of_var", [P, G])
        inverse, newton = sb("inverse_root", [P, G]), sb("newton", [P, G])
        aff = sb("bn_affine", [P, 2, 2, G])
        qb = sb("proj_bias", [P, 1])
        gam = sb("gamma_signs", [P, 3])
        pro = sb("prototypes", [P, D])
        prosq = sb("prototypes_sq", [P, D])
        pn2 = sb("prototype_norms", [P, 2])

        banks = [ctx.enter_context(nc.psum_tensor(f"bank{i}", [P, BANK], fp32)) for i in range(8)]
        expert_ps = [(banks[0], banks[1]), (banks[2], banks[3])]
        q_ps = banks[4]

        params = sem("params_loaded")
        ident_cleared, ident_ready = sem("ident_cleared"), sem("ident_ready")
        cleared, norms_ready, weights_ready = sem("cleared"), sem("norms_ready"), sem("weights_ready")
        stack_cleared = sem("stack_cleared")
        stack_in = [sem(f"stack_loaded{b}") for b in range(BLOCKS0)]
        x1_in = [sem(f"x1_loaded{m}") for m in range(IMAGES)]
        stack_done, stack_copied = sem("stack_done"), sem("stack_copied")
        block_summed, block_mean, block_squared = sem("block_summed"), sem("block_mean"), sem("block_squared")
        blocks_kept = sem("blocks_kept")
        conv0_out = [sem(f"conv0_stored{b}") for b in range(BLOCKS0)]
        conv1_out = [sem(f"conv1_stored{m}") for m in range(IMAGES)]
        setup, norm_step = sem("setup_steps"), sem("norm_steps")
        tap_added, mean_ready = sem("tap_added"), sem("image_mean_ready")
        image_summed, stats1_kept = sem("image_summed"), sem("stats1_kept")
        junk_written = sem("junk_written")
        body_aggregated, stats2_kept = sem("body_aggregated"), sem("stats2_kept")
        blocks_out, blocks_in, blocks_ready = sem("block_stats_stored"), sem("block_stats_loaded"), sem("block_stats_ready")
        cross_ready, q_ready = sem("q_cross_ready"), sem("q_ready")
        turned, top_ready = sem("logits_turned"), sem("top_ready")
        total_ready, inverse_ready, expert_added = sem("total_ready"), sem("inverse_ready"), sem("expert_added")
        part_done, part_copied = sem("conv_part_done"), sem("conv_part_copied")
        conv_ready = sem("conv_ready")
        var_ready, root_ready, norm_ready = sem("var_ready"), sem("root_ready"), sem("norm_ready")
        conv_in = [sem(f"conv_loaded{i}") for i in range(SLOTS)]
        y_high, y_low = sem("y_high"), sem("y_low")
        q_done, qq_ready = sem("q_done"), sem("qq_ready")
        dist_done, logits_ready = sem("dist_done"), sem("logits_ready")
        centered_ready, exp_ready, gates_ready = sem("centered_ready"), sem("exp_ready"), sem("gates_ready")
        experts_done, mix_begun, mixed = sem("experts_done"), sem("mix_begun"), sem("mixed")
        transposed, mix_measured = sem("transposed"), sem("mix_measured")
        mix_out = [sem(f"mix_stored{i}") for i in range(SLOTS)]
        x_again = [sem(f"x_reloaded{i}") for i in range(RING)]
        mix_in = [sem(f"mix_reloaded{i}") for i in range(RING)]
        summed, out_ready = sem("residual_added"), sem("out_ready")
        out_stored = [sem(f"out_stored{i}") for i in range(RING)]

        block = ctx.enter_context(nc.Block())
        ITS1, ITS2, ITS3 = N // IMAGES, CHUNKS // SLOTS, UNITS // RING
        N_PARAM_DMAS = 17

        def staged(engine, its, body):
            body(0, False)
            body(1, False)
            with engine.Fori(2, its - 1) as it:
                body(it, False)
            body(its - 1, True)

        def i_bank(b, half):
            return 2 * (b % 2) + half

        @block.sync
        def _(sp):
            with nc.allow_non_contiguous_dma(reason="small parameters, once"):
                sp.dma_start(taps[:, :], dw[P:C, :]).then_inc(params, 16)
                for d in range(3):
                    sp.dma_start(stack_taps[32 * d:32 * d + 32],
                                 dw[0:P, 3 * d:3 * d + 3].rearrange("(b c) t -> c b t", c=32)).then_inc(params, 16)
                sp.dma_start(gam[:, 0:1], gamma.partition_broadcast(P)).then_inc(params, 16)
                for i, v in enumerate((bn1s, bn1b, bn2s, bn2b)):
                    sp.dma_start(bnp[:, i, :], v.rearrange("(g p) -> p g", g=G)).then_inc(params, 16)
                sp.dma_start(qb[D:P, :], projb.rearrange("(p a) -> p a", a=1)).then_inc(params, 16)
                sp.dma_start(pload, projT.rearrange("(k p) d -> p k d", k=G)).then_inc(params, 16)
                sp.dma_start(wload, expT.rearrange("(k p) n -> p k n", k=G)).then_inc(params, 16)
                sp.wait_ge(cleared, 1)
                sp.dma_start(to_dist[0:D, 0:E], protoT).then_inc(params, 16)
                for j in range(4):
                    sp.dma_start(pro[32 * j:32 * j + E, :], proto).then_inc(params, 16)

            def load_block(n, b):
                for d in range(3):
                    h0, h1 = span(d - 1, H)
                    sp.dma_start(stack[32 * d:32 * d + 32, b, h0 * W:h1 * W],
                                 x_units[n * G, 32 * b:32 * b + 32, (h0 + d - 1) * W:(h1 + d - 1) * W]
                                 ).then_inc(stack_in[b], 16)

            def load_group1(n, m):
                sp.dma_start(x1[:, m, :], x_units[n * G + 1]).then_inc(x1_in[m], 16)

            def store_group1(n, m):
                sp.wait_ge(conv_ready, n + 1)
                sp.dma_start(conv_images[1, n], conv1[:, m, :]).then_inc(conv1_out[m], 16)

            for b in range(BLOCKS0):
                load_block(0, b)
            load_group1(0, 0)

            def body1(it, last):
                for m in range(IMAGES):
                    n = IMAGES * it + m
                    more = not (last and m + 1 >= IMAGES)
                    for b in range(BLOCKS0):
                        sp.wait_ge(stack_copied, 2 * (BLOCKS0 * n + b + 1))
                        for a in range(4):
                            sp.dma_start(conv_quarters[0, n, b, a], conv0[32 * a:32 * a + 32, b, :]
                                         ).then_inc(conv0_out[b], 16)
                        if more:
                            load_block(n + 1, b)
                    if exists(n - 1):
                        store_group1(n - 1, (m - 1) % IMAGES)
                    if more:
                        load_group1(n + 1, (m + 1) % IMAGES)
            staged(sp, ITS1, body1)
            store_group1(N - 1, IMAGES - 1)

            def blocks_to_dram(n, blocks):
                sp.wait_ge(blocks_ready, n + 1)
                sp.dma_start(blocks_dram[n], block_st[:, 0:blocks, :].rearrange("p b s -> p (b s)")
                             ).then_inc(blocks_out, 16)

            def blocks_from_dram(n, blocks):
                sp.wait_ge(blocks_out, 16 * (n + 1))
                with nc.allow_non_contiguous_dma(reason="small, once"):
                    for b in range(blocks):
                        sp.dma_start(channel_st[32 * (b % 4):32 * (b % 4) + 32, b // 4],
                                     blocks_dram[n][:, 3 * b:3 * b + 3].rearrange("(a i) s -> i a s", a=4)
                                     ).then_inc(blocks_in, 16)

            blocks_to_dram(0, BLOCKS0)
            for b in range(BLOCKS0):
                sp.wait_ge(conv0_out[b], 64 * N)
            for m in range(IMAGES):
                sp.wait_ge(conv1_out[m], 16 * ITS1)

            def load_chunk(c, slot):
                sp.dma_start(cv[:, slot], conv_chunks[c]).then_inc(conv_in[slot], 16)

            for c in range(SLOTS - 1):
                load_chunk(c, c)
            blocks_from_dram(0, BLOCKS0)

            def load_x(n, g, slot):
                sp.dma_start(yb[:, slot, :], x_units[n * G + g]).then_inc(x_again[slot], 16)

            sp.wait_ge(junk_written, 4 * N)
            for k in range(RING):
                load_x(k // G, k % G, k)

            def body2(it, last):
                for j in range(SLOTS):
                    c = SLOTS * it + j
                    if not (last and j + SLOTS - 1 >= SLOTS):
                        wait(sp, y_high, c)
                        load_chunk(c + SLOTS - 1, (j + SLOTS - 1) % SLOTS)
                    sp.wait_ge(transposed, TILES * (c + 1))
                    for a in range(4):
                        sp.dma_start(mix_blocks[c, a], mo[32 * a:32 * a + 32, j // 2, :, j % 2]).then_inc(mix_out[j], 16)
            staged(sp, ITS2, body2)

            for j in range(SLOTS):
                sp.wait_ge(mix_out[j], 64 * ITS2)
            sp.wait_ge(mix_measured, CHUNKS)
            blocks_to_dram(1, BLOCKS)
            blocks_from_dram(1, BLOCKS)

            def load_mix(n, g, slot):
                sp.dma_start(xb[:, slot, :], mix_units[n, g]).then_inc(mix_in[slot], 16)

            def load_pair(n, g, slot):
                load_x(n, g, slot)
                load_mix(n, g, slot)

            for k in range(RING - 1):
                load_mix(k // G, k % G, k)

            def body3(it, last):
                for k in range(RING):
                    u = RING * it + k
                    ahead = k + RING - 1
                    slot = ahead % RING
                    sp.wait_ge(out_ready, u + 1)
                    sp.dma_start(out_units[u], xb[:, k, :]).then_inc(out_stored[k], 16)
                    if not (last and ahead >= RING):
                        wait(sp, out_stored[slot], 16 * (it + ahead // RING))
                        if isinstance(u, int) and u == 0:
                            load_mix(ahead // G, ahead % G, slot)
                        else:
                            load_pair(2 * it + ahead // G, ahead % G, slot)
            staged(sp, ITS3, body3)
            for k in range(RING):
                sp.wait_ge(out_stored[k], 16 * ITS3)

        @block.gpsimd
        def _(pool):
            nc.gpsimd.memset(ident[:, :], 0.0).then_inc(ident_cleared, 1)
            pool.wait_ge(ident_cleared, 1)
            nc.gpsimd.affine_select(out=ident[:, :], in_=ident[:, :], compare_op=ALU.not_equal, fill=1.0, base=0,
                                    pattern=[[-1, P]], channel_multiplier=1).then_inc(ident_ready, 1)

            def body2(it, last):
                for j in range(SLOTS):
                    c = SLOTS * it + j
                    pool.wait_ge(y_high, c + 1)
                    nc.gpsimd.tensor_tensor(yl[:, j], y32[:, j % 2], yh[:, j].bitcast(fp32),
                                            ALU.subtract).then_inc(y_low, 1)
            staged(pool, ITS2, body2)

        @block.scalar
        def _(act):
            act.wait_ge(params, 16 * N_PARAM_DMAS)
            nc.scalar.activation(prosq[:, :], pro[:, :], ACT.Square, accum_out=pn2[:, 0:1]).then_inc(norms_ready, 1)

            def copy_block(n, it, m, b):
                wait(act, conv0_out[b], 64 * n)
                wait(act, block_squared, BLOCKS0 * (n - 1) + b + 1)
                for s_ in range(2):
                    i = 2 * (BLOCKS0 * n + b) + s_
                    act.wait_ge(stack_done, i + 1)
                    size = SUB_ROWS * W
                    nc.scalar.activation(conv0[:, b, s_ * size:(s_ + 1) * size], banks[i_bank(b, s_)][:, 0:size],
                                         ACT.Copy).then_inc(stack_copied, 1)

            def measure_block(n, m, b):
                i = BLOCKS0 * n + b
                if b == 0:
                    wait(act, blocks_kept, n - 1)
                act.wait_ge(stack_copied, 2 * (i + 1))
                wait(act, block_squared, i)
                nc.scalar.activation(junk0, conv0[:, b, :], ACT.Identity,
                                     accum_out=block_sum[:, m, b:b + 1]).then_inc(block_summed, 1)
                act.wait_ge(block_summed, i + 1)
                nc.scalar.activation(block_minus_mean[:, m, b:b + 1], block_sum[:, m, b:b + 1], ACT.Copy,
                                     scale=-1.0 / QUARTER).then_inc(block_mean, 1)
                act.wait_ge(block_mean, i + 1)
                nc.scalar.activation(junk0, conv0[:, b, :], ACT.Square, bias=block_minus_mean[:, m, b:b + 1],
                                     accum_out=block_squares[:, m, b:b + 1]).then_inc(block_squared, 1)

            def measure_image(n, m):
                act.wait_ge(conv_ready, n + 1)
                wait(act, stats1_kept, n - IMAGES + 1)
                for h in range(2):
                    wait(act, junk_written, 4 * n + h)
                    nc.scalar.activation(junk1, conv1[:, m, h * HALF:(h + 1) * HALF], ACT.Identity,
                                         accum_out=halves[:, m, 0, h:h + 1]).then_inc(junk_written, 1)
                act.wait_ge(junk_written, 4 * n + 2)
                nc.scalar.activation(image_sum[:, m:m + 1], halves[:, m, 0, 0:1], ACT.Identity,
                                     bias=halves[:, m, 0, 1:2]).then_inc(image_summed, 1)
                act.wait_ge(image_summed, n + 1)
                nc.scalar.activation(minus_mean[:, m:m + 1], image_sum[:, m:m + 1], ACT.Copy,
                                     scale=-1.0 / HW).then_inc(mean_ready, 1)
                act.wait_ge(mean_ready, n + 1)
                for h in range(2):
                    wait(act, junk_written, 4 * n + 2 + h)
                    nc.scalar.activation(junk1, conv1[:, m, h * HALF:(h + 1) * HALF], ACT.Square,
                                         bias=minus_mean[:, m:m + 1],
                                         accum_out=halves[:, m, 1, h:h + 1]).then_inc(junk_written, 1)

            def body1(it, last):
                for m in range(IMAGES):
                    n = IMAGES * it + m
                    for b in range(BLOCKS0):
                        copy_block(n, it, m, b)
                        if b < BLOCKS0 - 1:
                            measure_block(n, m, b)
                        if b == 1 and exists(n - IMAGES):
                            measure_image(n - IMAGES, m)
                    wait(act, conv1_out[m], 16 * it)
                    wait(act, junk_written, 4 * (n - 1))
                    for r in range(PARTS):
                        act.wait_ge(part_done, PARTS * n + r + 1)
                        nc.scalar.activation(conv1[:, m, r * ROWS * W:(r + 1) * ROWS * W],
                                             banks[4 + r % 4][:, 0:ROWS * W], ACT.Copy).then_inc(part_copied, 1)
                    measure_block(n, m, BLOCKS0 - 1)
            junk0 = mix[:, :, :].rearrange("p t n -> p (t n)")[:, 0:QUARTER]
            junk1 = y32[:, :, :, :].rearrange("p a g q -> p (a g q)")[:, 0:HALF]
            act.wait_ge(weights_ready, 1)
            staged(act, ITS1, body1)
            for m in range(IMAGES):
                measure_image(N - IMAGES + m, m)

            def root(n):
                act.wait_ge(var_ready, n + 1)
                nc.scalar.activation(root_of[:, :], var_eps[:, :], ACT.Sqrt).then_inc(root_ready, 1)
            root(0)
            act.wait_ge(norm_ready, 1)

            def relu(c, it, j, piece):
                if piece == 0:
                    act.wait_ge(conv_in[j % SLOTS], 16 * (it + 1 + j // SLOTS))
                    wait(act, y_low, c - 1)
                    wait(act, experts_done, 2 * TILES * (c - SLOTS + 1))
                g = piece // 2
                y = (y32[:, j % 2], yh[:, j % SLOTS])[piece % 2]
                done = nc.scalar.activation(y[:, g].rearrange("p (t a i) -> p a t i", t=TILES, i=32),
                                            cv[:, j % SLOTS, g].rearrange("p (a t i) -> p a t i", t=TILES, i=32),
                                            ACT.Relu,
                                            scale=aff[:, 0, 0, g:g + 1], bias=aff[:, 0, 1, g:g + 1])
                if piece == 3:
                    done.then_inc(y_high, 1)

            def cross(c, j):
                act.wait_ge(q_done, c + 1)
                wait(act, q_ready, c)
                nc.scalar.activation(q_cross[:, :], q_ps[D:P, :], ACT.Identity, bias=qb[D:P, :]).then_inc(cross_ready, 1)

            def square(c, j):
                act.wait_ge(q_ready, c + 1)
                nc.scalar.activation(qq[D:P, j % 2], qq[0:D, j % 2], ACT.Square).then_inc(qq_ready, 1)

            def logits(c, j):
                act.wait_ge(dist_done, c + 1)
                wait(act, centered_ready, c - 1)
                nc.scalar.activation(logit_rows[:, j % 2], q_ps[:, 0:P], ACT.Identity,
                                     scale=gam[:, 2:3], bias=pn2[:, 1:2]).then_inc(logits_ready, 1)

            def exps(c, j):
                act.wait_ge(centered_ready, c + 1)
                wait(act, gates_ready, c - 1)
                nc.scalar.activation(ex[:, j % 2], centered[:, j % 2], ACT.Exp).then_inc(exp_ready, 1)

            def begin_mix(c, j, t):
                if t == 0:
                    act.wait_ge(gates_ready, c + 1)
                act.wait_ge(experts_done, 2 * (TILES * c + t) + 1)
                wait(act, transposed, TILES * (c - 1) + t + 1)
                nc.scalar.activation(mix[:, t], expert_ps[t % 2][0][:, 0:COUT], ACT.Copy,
                                     scale=gate[:, j % 2, t, 0:1]).then_inc(mix_begun, 1)

            for c in range(2):
                for piece in range(4):
                    relu(c, 0, c, piece)
            cross(0, 0)
            square(0, 0)
            logits(0, 0)
            exps(0, 0)

            def body2(it, last):
                for j in range(SLOTS):
                    c = SLOTS * it + j
                    more, two_more = not (last and j + 1 >= SLOTS), not (last and j + 2 >= SLOTS)
                    begin_mix(c, j, 0)
                    if more:
                        cross(c + 1, j + 1)
                    if two_more:
                        relu(c + 2, it, j + 2, 0)
                        relu(c + 2, it, j + 2, 1)
                    if more:
                        square(c + 1, j + 1)
                    begin_mix(c, j, 1)
                    if two_more:
                        relu(c + 2, it, j + 2, 2)
                    begin_mix(c, j, 2)
                    if more:
                        logits(c + 1, j + 1)
                    if two_more:
                        relu(c + 2, it, j + 2, 3)
                    if more:
                        exps(c + 1, j + 1)
                    begin_mix(c, j, 3)
            staged(act, ITS2, body2)
            root(1)

            def body3(it, last):
                for k in range(RING):
                    act.wait_ge(summed, RING * it + k + 1)
                    nc.scalar.activation(xb[:, k, :], xb[:, k, :], ACT.Relu,
                                         bias=aff[:, 1, 1, k % G:k % G + 1]).then_inc(out_ready, 1)
            staged(act, ITS3, body3)

        @block.tensor
        def _(pe):
            pe.wait_ge(weights_ready, 1)

            pe.wait_ge(stack_cleared, 1)

            def stacked(n, b, s_):
                i = 2 * (BLOCKS0 * n + b) + s_
                wait(pe, stack_copied, i - 3)
                sums = banks[i_bank(b, s_)][:, 0:SUB_ROWS * W].rearrange("p (h w) -> p h w", w=W)
                image = stack[:, b, :].rearrange("p (h w) -> p h w", w=W)
                for d, dx in enumerate((0, -1, 1)):
                    w0, w1 = span(dx, W)
                    for a in range(4):
                        h0 = a * Q_ROWS + s_ * SUB_ROWS
                        done = nc.tensor.matmul(sums[32 * a:32 * a + 32, :, w0:w1], stack_w[:, b, dx + 1, :],
                                                image[:, h0:h0 + SUB_ROWS, w0 + dx:w1 + dx],
                                                start=d == 0, stop=d == 2)
                done.then_inc(stack_done, 1)

            def diagonal(n, m, r):
                wait(pe, part_copied, PARTS * n + r - 3 if r >= 4 else PARTS * (n - 1) + (r + 5 if r < 3 else 4))
                image = x1[:, m, :].rearrange("p (h w) -> p h w", w=W)
                sums = banks[4 + r % 4][:, 0:ROWS * W].rearrange("p (h w) -> p h w", w=W)
                for i, (dy, dx) in enumerate(PE_TAPS[m]):
                    (h0, h1), (w0, w1) = span(dy, H), span(dx, W)
                    h0, h1 = max(h0, r * ROWS), min(h1, (r + 1) * ROWS)
                    done = nc.tensor.matmul(sums[:, h0 - r * ROWS:h1 - r * ROWS, w0:w1], diag[:, i, :],
                                            image[:, h0 + dy:h1 + dy, w0 + dx:w1 + dx],
                                            start=i == 0, stop=i == len(PE_TAPS[m]) - 1)
                done.then_inc(part_done, 1)

            def body1(it, last):
                for m in range(IMAGES):
                    n = IMAGES * it + m
                    for b in range(BLOCKS0):
                        pe.wait_ge(stack_in[b], 48 * (n + 1))
                        for s_ in range(2):
                            stacked(n, b, s_)
                    pe.wait_ge(x1_in[m], 16 * (it + 1))
                    for r in range(PARTS):
                        diagonal(n, m, r)
            staged(pe, ITS1, body1)

            def project(c, j):
                pe.wait_ge(y_low, c + 1)
                wait(pe, logits_ready, c)
                passes = [(w, y, k) for k in range(G) for w, y in ((proj_for_high, yh), (proj_for_low, yl))]
                for i, (w, y, k) in enumerate(passes):
                    done = nc.tensor.matmul(q_ps[:, :], w[:, k, :], y[:, j % SLOTS, k, :],
                                            start=i == 0, stop=i == len(passes) - 1)
                done.then_inc(q_done, 1)

            def distances(c, j):
                pe.wait_ge(qq_ready, c + 1)
                pixels = qq[:, j % 2, :].rearrange("p (t a i) -> p a t i", t=TILES, i=32)
                for a in range(4):
                    done = nc.tensor.matmul(q_ps[32 * a:32 * a + 32, 0:P], to_dist[:, :], pixels[:, a],
                                            start=True, stop=True)
                done.then_inc(dist_done, 1)

            def experts(c, j, t, halves=(0, 1)):
                for half in halves:
                    if half == 0:
                        wait(pe, expert_added, (E - 2) * (TILES * c + t - 2) + 1)
                    else:
                        wait(pe, mixed, TILES * c + t - 1)
                    passes = [(y, w, k) for k in range(G) for y, w in ((yh, wh), (yh, wl), (yl, wh))]
                    for i, (y, w, k) in enumerate(passes):
                        done = nc.tensor.matmul(expert_ps[t % 2][half][:, :], y[:, j, k, t * P:(t + 1) * P],
                                                w[:, k, half * BANK:(half + 1) * BANK],
                                                start=i == 0, stop=i == len(passes) - 1)
                    done.then_inc(experts_done, 1)

            pe.wait_ge(norm_ready, 1)
            project(0, 0)
            distances(0, 0)

            def body2(it, last):
                for j in range(SLOTS):
                    c = SLOTS * it + j
                    more = not (last and j + 1 >= SLOTS)
                    experts(c, j, 0)
                    if more:
                        project(c + 1, j + 1)
                    experts(c, j, 1)
                    experts(c, j, 2, (0,))
                    if more:
                        distances(c + 1, j + 1)
                    experts(c, j, 2, (1,))
                    experts(c, j, 3)
            staged(pe, ITS2, body2)

        @block.vector
        def _(dve):
            steps = [0]

            def then(instruction):
                instruction.then_inc(setup, 1)
                steps[0] += 1
                dve.wait_ge(setup, steps[0])

            nc.vector.memset(pro[:, :], 0.0)
            then(nc.vector.memset(to_dist[:, :], 0.0))
            nc.vector.memset(to_dist[D:P, 0:E], 1.0).then_inc(cleared, 1)
            nc.vector.memset(stack[0:32, :, 0:W], 0.0)
            nc.vector.memset(stack[64:96, :, HW - W:HW], 0.0)
            nc.vector.memset(stack[96:128, :, :], 0.0).then_inc(stack_cleared, 1)
            dve.wait_ge(params, 16 * N_PARAM_DMAS)
            dve.wait_ge(ident_ready, 1)
            for whole, high, low in ((wload, wh[:, :, :], wl[:, :, :]),
                                     (pload[:, :, 0:D], proj_for_high[:, :, 0:D], proj_for_high[:, :, D:2 * D])):
                then(nc.vector.tensor_copy(high, whole))
                nc.vector.tensor_tensor(low, whole, high.bitcast(fp32), ALU.subtract)
            nc.vector.memset(proj_for_low[:, :, 0:D].bitcast(fp32), 0.0)
            nc.vector.tensor_copy(proj_for_low[:, :, D:2 * D], pload[:, :, 0:D])
            nc.vector.memset(st0[:, :, :, :, 0], float(QUARTER))
            nc.vector.memset(st1[:, :, :, 0], float(HW))
            then(nc.vector.memset(stack_w[:, :, :, :], 0.0))
            nc.vector.tensor_scalar(to_dist[0:D, 0:E], to_dist[0:D, 0:E], -2.0, None, ALU.mult)
            then(nc.vector.tensor_scalar(gam[:, 1:2], gam[:, 0:1], -1.0, None, ALU.mult))
            then(nc.vector.tensor_tensor(gam[:, 2:3], gam[:, 0:1], gam[:, 1:2], ALU.min))
            dve.wait_ge(norms_ready, 1)
            nc.vector.tensor_tensor(pn2[:, 1:2], pn2[:, 0:1], gam[:, 2:3], ALU.mult)
            for d in range(3):
                own = slice(32 * d, 32 * d + 32)
                for b in range(BLOCKS0):
                    for dx in range(3):
                        nc.vector.tensor_scalar(stack_w[own, b, dx, :], ident[own, own],
                                                stack_taps[own, b, dx:dx + 1], None, ALU.mult)
            for i, (dy, dx) in enumerate(max(PE_TAPS, key=len)):
                done = nc.vector.tensor_scalar(diag[:, i, :], ident[:, :], taps[:, tap(dy, dx):tap(dy, dx) + 1],
                                               None, ALU.mult)
            done.then_inc(weights_ready, 1)

            def body1(it, last):
                between = [len(taps_) - 1 for taps_ in DVE_TAPS]
                for m in range(IMAGES):
                    n = IMAGES * it + m
                    dve.wait_ge(part_copied, PARTS * (n + 1))
                    image = x1[:, m, :].rearrange("p (h w) -> p h w", w=W)
                    sums = conv1[:, m, :].rearrange("p (h w) -> p h w", w=W)
                    for i, (dy, dx) in enumerate(DVE_TAPS[m]):
                        if i:
                            dve.wait_ge(tap_added, sum(between) * it + sum(between[:m]) + i)
                        (h0, h1), (w0, w1) = span(dy, H), span(dx, W)
                        onto = sums[:, h0:h1, w0:w1]
                        done = nc.vector.scalar_tensor_tensor(
                            out=onto, in0=image[:, h0 + dy:h1 + dy, w0 + dx:w1 + dx],
                            scalar=taps[:, tap(dy, dx):tap(dy, dx) + 1], in1=onto, op0=ALU.mult, op1=ALU.add)
                        done.then_inc(tap_added if i < between[m] else conv_ready, 1)
                    keep_blocks(n, it, m)
                    if exists(n - IMAGES):
                        keep_image(n - IMAGES, it - 1, m)

            def keep_blocks(n, it, m):
                dve.wait_ge(block_squared, BLOCKS0 * (n + 1))
                nc.vector.tensor_scalar(st0[:, it, m, :, 1], block_minus_mean[:, m, :], -1.0, None, ALU.mult)
                nc.vector.tensor_copy(st0[:, it, m, :, 2], block_squares[:, m, :]).then_inc(blocks_kept, 1)

            def keep_image(n, it, m):
                dve.wait_ge(junk_written, 4 * (n + 1))
                nc.vector.tensor_scalar(st1[:, it, m, 1:2], minus_mean[:, m:m + 1], -1.0, None, ALU.mult)
                nc.vector.tensor_tensor(st1[:, it, m, 2:3], halves[:, m, 1, 0:1], halves[:, m, 1, 1:2],
                                        ALU.add).then_inc(stats1_kept, 1)
            staged(dve, ITS1, body1)
            norm_steps = [0]

            def step(instruction):
                instruction.then_inc(norm_step, 1)
                norm_steps[0] += 1
                dve.wait_ge(norm_step, norm_steps[0])

            def normalise(n):
                nc.vector.tensor_scalar(var_eps[:, :], mv[:, :, 1], EPS, None, ALU.add).then_inc(var_ready, 1)
                dve.wait_ge(root_ready, n + 1)
                step(nc.vector.reciprocal(inverse[:, :], root_of[:, :]))
                step(nc.vector.tensor_tensor(newton[:, :], inverse[:, :], inverse[:, :], ALU.mult))
                step(nc.vector.tensor_tensor(newton[:, :], newton[:, :], var_eps[:, :], ALU.mult))
                step(nc.vector.tensor_scalar(newton[:, :], newton[:, :], -0.5, 1.5, ALU.mult, ALU.add))
                step(nc.vector.tensor_tensor(inverse[:, :], inverse[:, :], newton[:, :], ALU.mult))
                step(nc.vector.tensor_tensor(aff[:, n, 0], inverse[:, :], bnp[:, 2 * n], ALU.mult))
                step(nc.vector.tensor_tensor(newton[:, :], mv[:, :, 0], aff[:, n, 0], ALU.mult))
                nc.vector.tensor_tensor(aff[:, n, 1], bnp[:, 2 * n + 1], newton[:, :],
                                        ALU.subtract).then_inc(norm_ready, 1)
            def combine_blocks(stats, blocks, count):
                for b in range(blocks):
                    done = nc.vector.bn_aggr(block_mv[:, b, :], stats(b))
                step(done)
                nc.vector.memset(block_st[:, 0:blocks, 0], float(count))
                nc.vector.tensor_copy(block_st[:, 0:blocks, 1], block_mv[:, 0:blocks, 0])
                nc.vector.tensor_scalar(block_st[:, 0:blocks, 2], block_mv[:, 0:blocks, 1], float(count), None,
                                        ALU.mult).then_inc(blocks_ready, 1)

            dve.wait_ge(blocks_kept, N)
            combine_blocks(lambda b: st0[:, :, :, b, :].rearrange("p i m s -> p (i m) s"), BLOCKS0, N * QUARTER)
            for m in range(IMAGES):
                keep_image(N - IMAGES + m, ITS1 - 1, m)
            dve.wait_ge(stats1_kept, N)
            step(nc.vector.bn_aggr(mv[:, 1, :], st1[:, :, :, :].rearrange("p i m s -> p (i m) s")))
            dve.wait_ge(blocks_in, 16 * BLOCKS0)
            step(nc.vector.bn_aggr(mv[:, 0, :], channel_st[:, 0]))
            normalise(0)

            def sum_q(c, j):
                dve.wait_ge(cross_ready, c + 1)
                wait(dve, dist_done, c - 1)
                nc.vector.tensor_tensor(qq[0:D, j % 2], q_ps[0:D, :], q_cross[:, :], ALU.add).then_inc(q_ready, 1)

            def turn(c, j):
                dve.wait_ge(logits_ready, c + 1)
                wait(dve, centered_ready, c)
                nc.vector.transpose(logit_t[:, :, :].rearrange("p t e -> p (t e)"),
                                    logit_rows[:, j % 2]).then_inc(turned, 1)

            def find_top(c, j):
                dve.wait_ge(turned, c + 1)
                nc.vector.tensor_reduce(out=top[:, :], in_=logit_t[:, :, 0:E], axis=AX.X,
                                        op=ALU.max).then_inc(top_ready, 1)

            def center(c, j):
                dve.wait_ge(top_ready, c + 1)
                nc.vector.tensor_tensor(centered[:, j % 2], logit_t[:, :, 0:E],
                                        top[:, :].unsqueeze(2).broadcast_to([P, TILES, E]),
                                        ALU.subtract).then_inc(centered_ready, 1)

            def sum_exps(c, j):
                dve.wait_ge(exp_ready, c + 1)
                wait(dve, gates_ready, c)
                nc.vector.tensor_reduce(out=total[:, :], in_=ex[:, j % 2], axis=AX.X,
                                        op=ALU.add).then_inc(total_ready, 1)

            def invert(c, j):
                dve.wait_ge(total_ready, c + 1)
                nc.vector.reciprocal(inv_total[:, :], total[:, :]).then_inc(inverse_ready, 1)

            def gates(c, j):
                dve.wait_ge(inverse_ready, c + 1)
                wait(dve, mixed, TILES * (c - 1))
                nc.vector.tensor_tensor(gate[:, j % 2], ex[:, j % 2],
                                        inv_total[:, :].unsqueeze(2).broadcast_to([P, TILES, E]),
                                        ALU.mult).then_inc(gates_ready, 1)

            def add_expert(c, j, t, e):
                if e == 1:
                    dve.wait_ge(mix_begun, TILES * c + t + 1)
                else:
                    dve.wait_ge(expert_added, (E - 2) * (TILES * c + t) + e - 1)
                if e == 2:
                    dve.wait_ge(experts_done, 2 * (TILES * c + t + 1))
                nc.vector.scalar_tensor_tensor(
                    out=mix[:, t], in0=expert_ps[t % 2][e // 2][:, (e % 2) * COUT:(e % 2 + 1) * COUT],
                    scalar=gate[:, j % 2, t, e:e + 1], in1=mix[:, t],
                    op0=ALU.mult, op1=ALU.add).then_inc(expert_added if e < E - 1 else mixed, 1)

            def transpose(c, it, j, t):
                dve.wait_ge(mixed, TILES * c + t + 1)
                if t == 0:
                    wait(dve, mix_out[j], 64 * it)
                    if j % 2 == 0:
                        wait(dve, mix_measured, c - 2)
                nc.vector.transpose(mo[:, j // 2, :, j % 2, t * 32:(t + 1) * 32],
                                    mix[:, t].rearrange("p (b q) -> p b q", q=32)).then_inc(transposed, 1)

            def measure(c, it, j, t):
                if j == 2 and t == 0:
                    wait(dve, stats2_kept, it)
                if t == 0:
                    dve.wait_ge(transposed, TILES * (c - j % 2))
                pair, b = 1 - j // 2, 4 * (j % 2) + t
                done = nc.vector.bn_stats(st2[:, pair, b, :], mo[:, pair, b].rearrange("p r q -> p (r q)"))
                if t == TILES - 1:
                    done.then_inc(mix_measured, 1)

            def aggregate(it):
                dve.wait_ge(mix_measured, SLOTS * (it + 1))
                nc.vector.tensor_scalar(st2_all[:, it, :, 0], st2[:, 0, :, 0], float(SLOTS), None, ALU.mult)
                for b in range(BLOCKS):
                    done = nc.vector.bn_aggr(body_mv[:, b, :], st2[:, :, b, :])
                done.then_inc(body_aggregated, 1)
                dve.wait_ge(body_aggregated, it + 1)
                nc.vector.tensor_copy(st2_all[:, it, :, 1], body_mv[:, :, 0])
                nc.vector.tensor_scalar(st2_all[:, it, :, 2], body_mv[:, :, 1], float(SLOTS * P), None,
                                        ALU.mult).then_inc(stats2_kept, 1)

            sum_q(0, 0)
            for step_of_softmax in (turn, find_top, center, sum_exps, invert, gates):
                step_of_softmax(0, 0)

            def body2(it, last):
                for j in range(SLOTS):
                    c = SLOTS * it + j
                    more = not (last and j + 1 >= SLOTS)
                    soon = [[], [], [turn, find_top, center], [sum_exps, invert, gates]]
                    for t in range(TILES):
                        steps = soon[t] if more else []
                        for e in range(1, E):
                            add_expert(c, j, t, e)
                            if steps:
                                steps[e - 1](c + 1, j + 1)
                            if e == 1 and t:
                                transpose(c, it, j, t - 1)
                            elif e == 1 and exists(c - 1):
                                transpose(c - 1, it if j else it - 1, (j - 1) % SLOTS, TILES - 1)
                            if e == 2 and exists(c - 2):
                                measure(c, it, j, t)
                        if t == 0 and more:
                            sum_q(c + 1, j + 1)
                    if j == 1 and exists(it - 1):
                        aggregate(it - 1)
            staged(dve, ITS2, body2)
            transpose(CHUNKS - 1, ITS2 - 1, SLOTS - 1, TILES - 1)
            for j in range(2):
                for t in range(TILES):
                    measure(CHUNKS + j, ITS2, j, t)
            aggregate(ITS2 - 1)
            dve.wait_ge(stats2_kept, ITS2)
            combine_blocks(lambda b: st2_all[:, :, b, :], BLOCKS, CHUNKS * 32 * TILES)
            dve.wait_ge(blocks_in, 16 * (BLOCKS0 + BLOCKS))
            for g in range(G):
                step(nc.vector.bn_aggr(mv[:, g, :], channel_st[:, g]))
            normalise(1)

            def body3(it, last):
                for k in range(RING):
                    dve.wait_ge(x_again[k], 16 * (it + 1))
                    dve.wait_ge(mix_in[k], 16 * (it + 1))
                    nc.vector.scalar_tensor_tensor(out=xb[:, k, :], in0=xb[:, k, :],
                                                   scalar=aff[:, 1, 0, k % G:k % G + 1], in1=yb[:, k, :],
                                                   op0=ALU.mult, op1=ALU.add).then_inc(summed, 1)
            staged(dve, ITS3, body3)


def kernel(**inputs):
    import numpy as np
    import concourse.bacc as bacc
    from concourse.bass_utils import run_bass_kernel_spmd

    arr = {k.replace("L0_conv_", ""): np.asarray(v) for k, v in inputs.items()}
    laid = {
        "x": arr["x"],
        "dw": arr["dw_w"].reshape(C, 9),
        "bn1s": arr["bn1_scale"], "bn1b": arr["bn1_bias"],
        "projT": arr["proj_w"].T, "projb": arr["proj_b"],
        "proto": arr["prototypes"], "protoT": arr["prototypes"].T,
        "gamma": arr["gamma"].reshape(1),
        "expT": arr["expert_w"].transpose(2, 0, 1).reshape(C, E * COUT),
        "bn2s": arr["bn2_scale"], "bn2b": arr["bn2_bias"],
    }
    laid = {k: np.ascontiguousarray(v) for k, v in laid.items()}
    nc = bacc.Bacc("TRN2", target_bir_lowering=False, num_devices=1)
    args = [nc.dram_tensor(f"in_{k}", v.shape, mybir.dt.from_np(v.dtype), kind="ExternalInput").ap() for k, v in laid.items()]
    out = nc.dram_tensor("out", (N, COUT, H, W), fp32, kind="ExternalOutput").ap()
    build(nc, *args, out)
    result = run_bass_kernel_spmd(nc, [{f"in_{k}": v for k, v in laid.items()}], core_ids=[0])
    return result.results[0]["out"]
```

```python
from contextlib import ExitStack

import concourse.bass as bass
from concourse import mybir

fp32 = mybir.dt.float32
f32r = mybir.dt.float32r
ALU = mybir.AluOpType
ACT = mybir.ActivationFunctionType
AX = mybir.AxisListType

N, C, H, W = 32, 256, 56, 56
E, D, COUT = 4, 64, 256
EPS = 1e-5
P = 128
G = C // P
HW = H * W
PIX = N * HW

IMAGES = 2
BLOCKS0 = P // 32
QUARTER = HW // 4
Q_ROWS = H // 4
SUB_ROWS = Q_ROWS // 2
ROWS = 8
PARTS = H // ROWS
TAPS = [(dy, dx) for dy in (-1, 0, 1) for dx in (-1, 0, 1)]
PE_TAPS = [[(0, 0)], [(0, 0), (-1, 0)]]
LAST_PE_TAPS = [(0, 0), (-1, 0), (1, 0)]
HALF = HW // 2

UNITS = N * G
RING = 4
LAST = UNITS - 1


def slots_of(last):
    return (*range(RING - 2), LAST, RING - 2) if last else range(RING)

TILES = 4
CH = TILES * P
CHUNKS = PIX // CH
SLOTS = 4
BANK = 512
BLOCKS = COUT // 32
MO_FROM = 3 * HW - 4 * BLOCKS * P
assert SLOTS * G * CH <= MO_FROM and 2 * HW <= MO_FROM + 2 * BLOCKS * P


def tap(dy, dx):
    return 3 * (dy + 1) + dx + 1


def pe_taps(m, last):
    return LAST_PE_TAPS if last and m == IMAGES - 1 else PE_TAPS[m]


def dve_taps(m, last):
    return [t for t in TAPS if t not in pe_taps(m, last)]


def group1_after(m, last):
    return 1 if last and m == IMAGES - 1 else BLOCKS0 - 1


def span(d, n):
    return max(0, -d), min(n, n - d)


def wait(engine, sem, value):
    if isinstance(value, int) and value <= 0:
        return
    engine.wait_ge(sem, value)


def exists(unit):
    return not isinstance(unit, int) or unit >= 0


def build(nc, x, dw, bn1s, bn1b, projT, projb, proto, protoT, gamma, expT, bn2s, bn2b, out):
    conv = nc.dram_tensor("conv_scratch", (G, P, PIX), fp32, kind="Internal").ap()
    mixd = nc.dram_tensor("mixed_scratch", (G, P, PIX), fp32, kind="Internal").ap()
    x_units = x.rearrange("n (g p) h w -> (n g) p (h w)", g=G)
    out_units = out.rearrange("n (g p) h w -> (n g) p (h w)", g=G)
    conv_images = conv.rearrange("g p (n q) -> g n p q", n=N)
    conv_quarters = conv.rearrange("g (b c) (n a q) -> g n b a c q", c=32, n=N, a=4)
    mix_units = mixd.rearrange("g p (n q) -> n g p q", n=N)
    conv_chunks = conv.rearrange("g p (c q) -> c p g q", q=CH)
    mix_blocks = mixd.rearrange("g (h i) (c a q) -> c a i (g h) q", i=32, a=4, q=P)
    blocks_dram = [nc.dram_tensor(f"block_stats{n}", (P, blocks * 3), fp32, kind="Internal").ap()
                   for n, blocks in enumerate((BLOCKS0, BLOCKS))]

    ctx = ExitStack()
    with ctx:
        def sb(name, shape, dt=fp32):
            return ctx.enter_context(nc.sbuf_tensor(name, shape, dt))

        def sem(name):
            return ctx.enter_context(nc.semaphore(name))

        xb = sb("stack_and_mixture_ring", [P, RING, HW])
        yb = sb("group1_and_x_ring", [P, RING, HW])
        stack = xb
        conv1, x1 = yb[:, 0:IMAGES], yb[:, IMAGES:2 * IMAGES]
        conv0 = sb("conv_blocks", [P, BLOCKS0, QUARTER])
        stack_w = sb("stack_weights", [P, BLOCKS0, 3, 32])
        stack_taps = sb("stack_taps", [P, BLOCKS0, 3])
        ring = xb[:, :, :].rearrange("p r q -> p (r q)")
        cv = ring[:, 0:SLOTS * G * CH].rearrange("p (s g q) -> p s g q", s=SLOTS, g=G)
        mo = ring[:, MO_FROM:3 * HW].rearrange("p (s b r q) -> p s b r q", s=2, b=BLOCKS, r=2)
        stage2 = sb("y_full_and_mix_ring", [P, HW])
        y32 = stage2[:, 0:2 * G * CH].rearrange("p (s g q) -> p s g q", s=2, g=G)
        mix = stage2[:, 2 * G * CH:2 * G * CH + TILES * COUT].rearrange("p (t n) -> p t n", t=TILES)
        yh = sb("y_high", [P, SLOTS, G, CH], f32r)
        yl = sb("y_low", [P, SLOTS, G, CH], f32r)
        last_x = sb("x_of_last_unit", [P, HW])
        last_mix = stage2[:, :]
        wload = yb[:, 0, 0:G * E * COUT].rearrange("p (k n) -> p k n", k=G)
        pload = yb[:, 1, 0:G * D].rearrange("p (k n) -> p k n", k=G)
        wh = sb("experts_high", [P, G, E * COUT], f32r)
        wl = sb("experts_low", [P, G, E * COUT], f32r)
        proj_for_high = sb("proj_high_low", [P, G, 2 * D], f32r)
        proj_for_low = sb("proj_none_high", [P, G, 2 * D], f32r)
        q_cross = sb("q_cross", [D, CH])
        qq = sb("q_and_square", [P, 2, CH])
        to_dist = sb("to_dist", [P, 32])
        logit_rows = sb("logit_rows", [P, 2, P])
        logit_t = sb("logit_pixels", [P, TILES, 32])
        top = sb("top_logit", [P, TILES])
        centered = sb("centered", [P, 2, TILES, E])
        ex = sb("exps", [P, 2, TILES, E])
        total = sb("exp_sum", [P, TILES])
        inv_total = sb("exp_sum_inverse", [P, TILES])
        gate = sb("gates", [P, 2, TILES, E])
        ident = sb("identity", [P, P])
        diag = sb("tap_diagonals", [P, len(LAST_PE_TAPS), P])
        taps = sb("taps", [P, 9])
        halves = sb("half_sums", [P, IMAGES, 2, 2])
        image_sum = sb("image_sum", [P, IMAGES])
        minus_mean = sb("image_minus_mean", [P, IMAGES])
        block_sum = sb("block_sum", [P, IMAGES, BLOCKS0])
        block_minus_mean = sb("block_minus_mean", [P, IMAGES, BLOCKS0])
        block_squares = sb("block_squares", [P, IMAGES, BLOCKS0])
        st0 = sb("stats_group0", [P, N // IMAGES, IMAGES, BLOCKS0, 3])
        st1 = sb("stats_group1", [P, N // IMAGES + PARTS, IMAGES, 3])
        st1_flat = st1[:, :, :, :].rearrange("p i m s -> p (i m) s")
        st2 = sb("stats2_now", [P, 2, BLOCKS, 6])
        body_mv = sb("body_mean_var", [P, BLOCKS, 2])
        st2_all = sb("stats2", [P, CHUNKS // SLOTS, BLOCKS, 3])
        block_mv = sb("block_mean_var", [P, BLOCKS, 2])
        block_st = sb("block_stats_out", [P, BLOCKS, 3])
        channel_st = sb("channel_stats", [P, G, 4, 3])
        bnp = sb("bn_params", [P, 4, G])
        mv = sb("mean_var", [P, G, 2])
        var_eps, root_of = sb("var_eps", [P, G]), sb("root_of_var", [P, G])
        inverse, newton = sb("inverse_root", [P, G]), sb("newton", [P, G])
        aff = sb("bn_affine", [P, 2, 2, G])
        qb = sb("proj_bias", [P, 1])
        gam = sb("gamma_signs", [P, 3])
        pro = sb("prototypes", [P, D])
        prosq = sb("prototypes_sq", [P, D])
        pn2 = sb("prototype_norms", [P, 2])

        banks = [ctx.enter_context(nc.psum_tensor(f"bank{i}", [P, BANK], fp32)) for i in range(8)]
        expert_ps = [(banks[0], banks[1]), (banks[2], banks[3])]
        q_ps = banks[4]

        params, taps_in = sem("params_loaded"), sem("taps_loaded")
        ident_cleared, ident_ready = sem("ident_cleared"), sem("ident_ready")
        cleared, norms_ready = sem("cleared"), sem("norms_ready")
        taps_ready, weights_ready = sem("tap_weights_ready"), sem("weights_ready")
        edges_cleared, last_measured = sem("stack_edges_cleared"), sem("last_image_measured")
        stack_cleared = sem("stack_cleared")
        stack_in = [sem(f"stack_loaded{b}") for b in range(BLOCKS0)]
        x1_in = [sem(f"x1_loaded{m}") for m in range(IMAGES)]
        stack_done, stack_copied = sem("stack_done"), sem("stack_copied")
        block_summed, block_mean, block_squared = sem("block_summed"), sem("block_mean"), sem("block_squared")
        blocks_kept = sem("blocks_kept")
        conv0_out = [sem(f"conv0_stored{b}") for b in range(BLOCKS0)]
        conv1_out = [sem(f"conv1_stored{m}") for m in range(IMAGES)]
        setup, norm_step = sem("setup_steps"), sem("norm_steps")
        tap_added, mean_ready = sem("tap_added"), sem("image_mean_ready")
        image_summed, stats1_kept = sem("image_summed"), sem("stats1_kept")
        junk_written = sem("junk_written")
        body_aggregated, stats2_kept = sem("body_aggregated"), sem("stats2_kept")
        blocks_out, blocks_in, blocks_ready = sem("block_stats_stored"), sem("block_stats_loaded"), sem("block_stats_ready")
        cross_ready, q_ready = sem("q_cross_ready"), sem("q_ready")
        turned, top_ready = sem("logits_turned"), sem("top_ready")
        total_ready, inverse_ready, expert_added = sem("total_ready"), sem("inverse_ready"), sem("expert_added")
        part_done, part_copied = sem("conv_part_done"), sem("conv_part_copied")
        conv_ready = sem("conv_ready")
        var_ready, root_ready, norm_ready = sem("var_ready"), sem("root_ready"), sem("norm_ready")
        conv_in = [sem(f"conv_loaded{i}") for i in range(SLOTS)]
        y_high, y_low = sem("y_high"), sem("y_low")
        q_done, qq_ready = sem("q_done"), sem("qq_ready")
        dist_done, logits_ready = sem("dist_done"), sem("logits_ready")
        centered_ready, exp_ready, gates_ready = sem("centered_ready"), sem("exp_ready"), sem("gates_ready")
        experts_done, mix_begun, mixed = sem("experts_done"), sem("mix_begun"), sem("mixed")
        transposed, mix_measured = sem("transposed"), sem("mix_measured")
        mix_out = [sem(f"mix_stored{i}") for i in range(SLOTS)]
        x_again = [sem(f"x_reloaded{i}") for i in range(RING)]
        mix_in = [sem(f"mix_reloaded{i}") for i in range(RING)]
        last_x_in, last_mix_in, last_stored = sem("last_x_loaded"), sem("last_mix_loaded"), sem("last_unit_stored")
        summed, out_ready = sem("residual_added"), sem("out_ready")
        out_stored = [sem(f"out_stored{i}") for i in range(RING)]

        block = ctx.enter_context(nc.Block())
        ITS1, ITS2, ITS3 = N // IMAGES, CHUNKS // SLOTS, UNITS // RING
        N_TAP_DMAS, N_PARAM_DMAS = 4, 13

        def staged(engine, its, body):
            body(0, False)
            body(1, False)
            with engine.Fori(2, its - 1) as it:
                body(it, False)
            body(its - 1, True)

        def i_bank(b, half):
            return 2 * (b % 2) + half

        @block.sync
        def _(sp):
            with nc.allow_non_contiguous_dma(reason="small parameters, once"):
                for d in range(3):
                    sp.dma_start(stack_taps[32 * d:32 * d + 32],
                                 dw[0:P, 3 * d:3 * d + 3].rearrange("(b c) t -> c b t", c=32)).then_inc(taps_in, 16)
                sp.dma_start(taps[:, :], dw[P:C, :]).then_inc(taps_in, 16)

            def load_block(n, b):
                for d in range(3):
                    h0, h1 = span(d - 1, H)
                    sp.dma_start(stack[32 * d:32 * d + 32, b, h0 * W:h1 * W],
                                 x_units[n * G, 32 * b:32 * b + 32, (h0 + d - 1) * W:(h1 + d - 1) * W]
                                 ).then_inc(stack_in[b], 16)

            load_block(0, 0)
            load_block(0, 1)
            with nc.allow_non_contiguous_dma(reason="small parameters, once"):
                sp.dma_start(gam[:, 0:1], gamma.partition_broadcast(P)).then_inc(params, 16)
                for i, v in enumerate((bn1s, bn1b, bn2s, bn2b)):
                    sp.dma_start(bnp[:, i, :], v.rearrange("(g p) -> p g", g=G)).then_inc(params, 16)
                sp.dma_start(qb[D:P, :], projb.rearrange("(p a) -> p a", a=1)).then_inc(params, 16)
                sp.dma_start(pload, projT.rearrange("(k p) d -> p k d", k=G)).then_inc(params, 16)
                sp.dma_start(wload, expT.rearrange("(k p) n -> p k n", k=G)).then_inc(params, 16)
                sp.wait_ge(cleared, 1)
                sp.dma_start(to_dist[0:D, 0:E], protoT).then_inc(params, 16)
                for j in range(4):
                    sp.dma_start(pro[32 * j:32 * j + E, :], proto).then_inc(params, 16)

            def load_group1(n, m):
                sp.dma_start(x1[:, m, :], x_units[n * G + 1]).then_inc(x1_in[m], 16)

            def store_group1(n, m):
                sp.wait_ge(conv_ready, n + 1)
                sp.dma_start(conv_images[1, n], conv1[:, m, :]).then_inc(conv1_out[m], 16)

            load_group1(0, 0)
            load_block(0, 2)
            load_block(0, 3)

            def body1(it, last):
                for m in range(IMAGES):
                    n = IMAGES * it + m
                    more = not (last and m + 1 >= IMAGES)
                    for b in range(BLOCKS0):
                        sp.wait_ge(stack_copied, 2 * (BLOCKS0 * n + b + 1))
                        for a in range(4):
                            sp.dma_start(conv_quarters[0, n, b, a], conv0[32 * a:32 * a + 32, b, :]
                                         ).then_inc(conv0_out[b], 16)
                        if more:
                            load_block(n + 1, b)
                        if b == (1 if last else BLOCKS0 - 1):
                            if exists(n - 1):
                                store_group1(n - 1, (m - 1) % IMAGES)
                            if more:
                                load_group1(n + 1, (m + 1) % IMAGES)
            staged(sp, ITS1, body1)

            def blocks_to_dram(n, blocks):
                sp.wait_ge(blocks_ready, n + 1)
                sp.dma_start(blocks_dram[n], block_st[:, 0:blocks, :].rearrange("p b s -> p (b s)")
                             ).then_inc(blocks_out, 16)

            def blocks_from_dram(n, blocks):
                sp.wait_ge(blocks_out, 16 * (n + 1))
                with nc.allow_non_contiguous_dma(reason="small, once"):
                    for b in range(blocks):
                        sp.dma_start(channel_st[32 * (b % 4):32 * (b % 4) + 32, b // 4],
                                     blocks_dram[n][:, 3 * b:3 * b + 3].rearrange("(a i) s -> i a s", a=4)
                                     ).then_inc(blocks_in, 16)

            def load_chunk(c, slot):
                sp.dma_start(cv[:, slot], conv_chunks[c]).then_inc(conv_in[slot], 16)

            assert (SLOTS - 1) * CH <= HW
            for b in range(BLOCKS0):
                sp.wait_ge(conv0_out[b], 64)
            sp.wait_ge(conv1_out[0], 16)
            for c in range(SLOTS - 1):
                load_chunk(c, c)
            blocks_to_dram(0, BLOCKS0)
            blocks_from_dram(0, BLOCKS0)
            store_group1(N - 1, IMAGES - 1)
            for b in range(BLOCKS0):
                sp.wait_ge(conv0_out[b], 64 * N)
            for m in range(IMAGES):
                sp.wait_ge(conv1_out[m], 16 * ITS1)

            def load_x(n, g, slot):
                sp.dma_start(yb[:, slot, :], x_units[n * G + g]).then_inc(x_again[slot], 16)

            def load_mix(n, g, slot):
                sp.dma_start(xb[:, slot, :], mix_units[n, g]).then_inc(mix_in[slot], 16)

            sp.wait_ge(junk_written, 4 * (N - 1))
            sp.wait_ge(last_measured, 1)

            def body2(it, last):
                for j in range(SLOTS):
                    c = SLOTS * it + j
                    if not (last and j + SLOTS - 1 >= SLOTS):
                        wait(sp, y_high, c)
                        load_chunk(c + SLOTS - 1, (j + SLOTS - 1) % SLOTS)
                    if isinstance(it, int) and it == 0:
                        load_x(j // G, j % G, j)
                    if isinstance(it, int) and it == 1 and j == 0:
                        sp.dma_start(last_x[:, :], x_units[LAST]).then_inc(last_x_in, 16)
                    if last and j == 2:
                        for stored in mix_out:
                            sp.wait_ge(stored, 64 * (ITS2 - 1))
                        load_mix(3 // G, 3 % G, 3)
                    if last and j == 3:
                        sp.wait_ge(y_high, CHUNKS)
                        load_mix(0, 0, 0)
                    sp.wait_ge(transposed, TILES * (c + 1))
                    for a in range(4):
                        sp.dma_start(mix_blocks[c, a], mo[32 * a:32 * a + 32, j // 2, :, j % 2]).then_inc(mix_out[j], 16)
            staged(sp, ITS2, body2)

            for j in range(2):
                sp.wait_ge(mix_out[j], 64 * ITS2)
            sp.wait_ge(mix_measured, CHUNKS - 2)
            load_mix(0, 1, 1)
            blocks_to_dram(1, BLOCKS)
            blocks_from_dram(1, BLOCKS)
            for j in range(2, SLOTS):
                sp.wait_ge(mix_out[j], 64 * ITS2)
            sp.wait_ge(mix_measured, CHUNKS)
            load_mix(1, 0, 2)
            sp.dma_start(last_mix, mix_units[LAST // G, LAST % G]).then_inc(last_mix_in, 16)

            def load_pair(n, g, slot):
                load_x(n, g, slot)
                load_mix(n, g, slot)

            def body3(it, last):
                for i, k in enumerate(slots_of(last)):
                    sp.wait_ge(out_ready, RING * it + i + 1)
                    if k == LAST:
                        sp.dma_start(out_units[LAST], last_mix).then_inc(last_stored, 16)
                        continue
                    sp.dma_start(out_units[RING * it + k], xb[:, k, :]).then_inc(out_stored[k], 16)
                    ahead = k + RING - 1
                    slot = ahead % RING
                    first = isinstance(it, int) and it == 0 and k == 0
                    if not first and not last:
                        wait(sp, out_stored[slot], 16 * (it + ahead // RING))
                        load_pair(2 * it + ahead // G, ahead % G, slot)
            staged(sp, ITS3, body3)
            for k in range(RING):
                sp.wait_ge(out_stored[k], 16 * (ITS3 if k < RING - 1 else ITS3 - 1))
            sp.wait_ge(last_stored, 16)

        @block.gpsimd
        def _(pool):
            nc.gpsimd.memset(ident[:, :], 0.0).then_inc(ident_cleared, 1)
            pool.wait_ge(ident_cleared, 1)
            nc.gpsimd.affine_select(out=ident[:, :], in_=ident[:, :], compare_op=ALU.not_equal, fill=1.0, base=0,
                                    pattern=[[-1, P]], channel_multiplier=1).then_inc(ident_ready, 1)
            pool.wait_ge(ident_ready, 1)
            for b in range(1, BLOCKS0):
                wait(pool, stack_cleared, b - 1)
                nc.gpsimd.memset(stack[96:128, b, :], 0.0).then_inc(stack_cleared, 1)
            pool.wait_ge(stack_cleared, BLOCKS0 - 1)

            def body2(it, last):
                for j in range(SLOTS):
                    c = SLOTS * it + j
                    pool.wait_ge(y_high, c + 1)
                    nc.gpsimd.tensor_tensor(yl[:, j], y32[:, j % 2], yh[:, j].bitcast(fp32),
                                            ALU.subtract).then_inc(y_low, 1)
            staged(pool, ITS2, body2)

        @block.scalar
        def _(act):
            act.wait_ge(params, 16 * N_PARAM_DMAS)
            nc.scalar.activation(prosq[:, :], pro[:, :], ACT.Square, accum_out=pn2[:, 0:1]).then_inc(norms_ready, 1)

            def copy_block(n, it, m, b):
                wait(act, conv0_out[b], 64 * n)
                wait(act, block_squared, BLOCKS0 * (n - 1) + b + 1)
                for s_ in range(2):
                    i = 2 * (BLOCKS0 * n + b) + s_
                    act.wait_ge(stack_done, i + 1)
                    size = SUB_ROWS * W
                    nc.scalar.activation(conv0[:, b, s_ * size:(s_ + 1) * size], banks[i_bank(b, s_)][:, 0:size],
                                         ACT.Copy).then_inc(stack_copied, 1)

            def measure_block(n, m, b):
                i = BLOCKS0 * n + b
                if b == 0:
                    wait(act, blocks_kept, n - 1)
                act.wait_ge(stack_copied, 2 * (i + 1))
                wait(act, block_squared, i)
                nc.scalar.activation(junk0, conv0[:, b, :], ACT.Identity,
                                     accum_out=block_sum[:, m, b:b + 1]).then_inc(block_summed, 1)
                act.wait_ge(block_summed, i + 1)
                nc.scalar.activation(block_minus_mean[:, m, b:b + 1], block_sum[:, m, b:b + 1], ACT.Copy,
                                     scale=-1.0 / QUARTER).then_inc(block_mean, 1)
                act.wait_ge(block_mean, i + 1)
                nc.scalar.activation(junk0, conv0[:, b, :], ACT.Square, bias=block_minus_mean[:, m, b:b + 1],
                                     accum_out=block_squares[:, m, b:b + 1]).then_inc(block_squared, 1)

            def measure_image(n, m):
                act.wait_ge(conv_ready, n + 1)
                wait(act, stats1_kept, n - IMAGES + 1)
                for h in range(2):
                    wait(act, junk_written, 4 * n + h)
                    nc.scalar.activation(junk1, conv1[:, m, h * HALF:(h + 1) * HALF], ACT.Identity,
                                         accum_out=halves[:, m, 0, h:h + 1]).then_inc(junk_written, 1)
                act.wait_ge(junk_written, 4 * n + 2)
                nc.scalar.activation(image_sum[:, m:m + 1], halves[:, m, 0, 0:1], ACT.Identity,
                                     bias=halves[:, m, 0, 1:2]).then_inc(image_summed, 1)
                act.wait_ge(image_summed, n + 1)
                nc.scalar.activation(minus_mean[:, m:m + 1], image_sum[:, m:m + 1], ACT.Copy,
                                     scale=-1.0 / HW).then_inc(mean_ready, 1)
                act.wait_ge(mean_ready, n + 1)
                for h in range(2):
                    wait(act, junk_written, 4 * n + 2 + h)
                    nc.scalar.activation(junk1, conv1[:, m, h * HALF:(h + 1) * HALF], ACT.Square,
                                         bias=minus_mean[:, m:m + 1],
                                         accum_out=halves[:, m, 1, h:h + 1]).then_inc(junk_written, 1)

            def copy_parts(n, it, m):
                wait(act, conv1_out[m], 16 * it)
                wait(act, junk_written, 4 * (n - 1))
                if isinstance(n, int) and n < IMAGES:
                    act.wait_ge(weights_ready, 1)
                for r in range(PARTS):
                    act.wait_ge(part_done, PARTS * n + r + 1)
                    nc.scalar.activation(conv1[:, m, r * ROWS * W:(r + 1) * ROWS * W],
                                         banks[4 + r % 4][:, 0:ROWS * W], ACT.Copy).then_inc(part_copied, 1)

            def body1(it, last):
                for m in range(IMAGES):
                    n = IMAGES * it + m
                    for b in range(BLOCKS0):
                        copy_block(n, it, m, b)
                        if b < BLOCKS0 - 1:
                            measure_block(n, m, b)
                        if b == 1 and exists(n - IMAGES):
                            measure_image(n - IMAGES, m)
                        if b == group1_after(m, last):
                            copy_parts(n, it, m)
                    measure_block(n, m, BLOCKS0 - 1)
            junk0 = mix[:, :, :].rearrange("p t n -> p (t n)")[:, 0:QUARTER]
            junk1 = y32[:, :, :, :].rearrange("p a g q -> p (a g q)")[:, 0:HALF]
            staged(act, ITS1, body1)
            measure_image(N - 2, 0)

            def root(n):
                act.wait_ge(var_ready, n + 1)
                nc.scalar.activation(root_of[:, :], var_eps[:, :], ACT.Sqrt).then_inc(root_ready, 1)
            root(0)
            act.wait_ge(norm_ready, 1)

            def relu(c, it, j, piece):
                if piece == 0:
                    act.wait_ge(conv_in[j % SLOTS], 16 * (it + 1 + j // SLOTS))
                    wait(act, y_low, c - 1)
                    wait(act, experts_done, 2 * TILES * (c - SLOTS + 1))
                g = piece // 2
                y = (y32[:, j % 2], yh[:, j % SLOTS])[piece % 2]
                done = nc.scalar.activation(y[:, g].rearrange("p (t a i) -> p a t i", t=TILES, i=32),
                                            cv[:, j % SLOTS, g].rearrange("p (a t i) -> p a t i", t=TILES, i=32),
                                            ACT.Relu,
                                            scale=aff[:, 0, 0, g:g + 1], bias=aff[:, 0, 1, g:g + 1])
                if piece == 3:
                    done.then_inc(y_high, 1)

            def cross(c, j):
                act.wait_ge(q_done, c + 1)
                wait(act, q_ready, c)
                nc.scalar.activation(q_cross[:, :], q_ps[D:P, :], ACT.Identity, bias=qb[D:P, :]).then_inc(cross_ready, 1)

            def square(c, j):
                act.wait_ge(q_ready, c + 1)
                nc.scalar.activation(qq[D:P, j % 2], qq[0:D, j % 2], ACT.Square).then_inc(qq_ready, 1)

            def logits(c, j):
                act.wait_ge(dist_done, c + 1)
                wait(act, centered_ready, c - 1)
                nc.scalar.activation(logit_rows[:, j % 2], q_ps[:, 0:P], ACT.Identity,
                                     scale=gam[:, 2:3], bias=pn2[:, 1:2]).then_inc(logits_ready, 1)

            def exps(c, j):
                act.wait_ge(centered_ready, c + 1)
                wait(act, gates_ready, c - 1)
                nc.scalar.activation(ex[:, j % 2], centered[:, j % 2], ACT.Exp).then_inc(exp_ready, 1)

            def begin_mix(c, j, t):
                if t == 0:
                    act.wait_ge(gates_ready, c + 1)
                act.wait_ge(experts_done, 2 * (TILES * c + t) + 1)
                wait(act, transposed, TILES * (c - 1) + t + 1)
                nc.scalar.activation(mix[:, t], expert_ps[t % 2][0][:, 0:COUT], ACT.Copy,
                                     scale=gate[:, j % 2, t, 0:1]).then_inc(mix_begun, 1)

            for c in range(2):
                for piece in range(4):
                    relu(c, 0, c, piece)
            cross(0, 0)
            square(0, 0)
            logits(0, 0)
            exps(0, 0)

            def body2(it, last):
                for j in range(SLOTS):
                    c = SLOTS * it + j
                    more, two_more = not (last and j + 1 >= SLOTS), not (last and j + 2 >= SLOTS)
                    begin_mix(c, j, 0)
                    if more:
                        cross(c + 1, j + 1)
                    if two_more:
                        relu(c + 2, it, j + 2, 0)
                        relu(c + 2, it, j + 2, 1)
                    if more:
                        square(c + 1, j + 1)
                    begin_mix(c, j, 1)
                    if two_more:
                        relu(c + 2, it, j + 2, 2)
                    begin_mix(c, j, 2)
                    if more:
                        logits(c + 1, j + 1)
                    if two_more:
                        relu(c + 2, it, j + 2, 3)
                    if more:
                        exps(c + 1, j + 1)
                    begin_mix(c, j, 3)
            staged(act, ITS2, body2)
            root(1)

            def body3(it, last):
                for i, k in enumerate(slots_of(last)):
                    act.wait_ge(summed, RING * it + i + 1)
                    sums = last_mix if k == LAST else xb[:, k, :]
                    nc.scalar.activation(sums, sums, ACT.Relu,
                                         bias=aff[:, 1, 1, k % G:k % G + 1]).then_inc(out_ready, 1)
            staged(act, ITS3, body3)

        @block.tensor
        def _(pe):
            pe.wait_ge(taps_ready, 1)
            pe.wait_ge(edges_cleared, 1)

            def stacked(n, b, s_):
                i = 2 * (BLOCKS0 * n + b) + s_
                wait(pe, stack_copied, i - 3)
                sums = banks[i_bank(b, s_)][:, 0:SUB_ROWS * W].rearrange("p (h w) -> p h w", w=W)
                image = stack[:, b, :].rearrange("p (h w) -> p h w", w=W)
                for d, dx in enumerate((0, -1, 1)):
                    w0, w1 = span(dx, W)
                    for a in range(4):
                        h0 = a * Q_ROWS + s_ * SUB_ROWS
                        done = nc.tensor.matmul(sums[32 * a:32 * a + 32, :, w0:w1], stack_w[:, b, dx + 1, :],
                                                image[:, h0:h0 + SUB_ROWS, w0 + dx:w1 + dx],
                                                start=d == 0, stop=d == 2)
                done.then_inc(stack_done, 1)

            def diagonal(n, m, r, on_pe):
                wait(pe, part_copied, PARTS * n + r - 3 if r >= 4 else PARTS * (n - 1) + (r + 5 if r < 3 else 4))
                image = x1[:, m, :].rearrange("p (h w) -> p h w", w=W)
                sums = banks[4 + r % 4][:, 0:ROWS * W].rearrange("p (h w) -> p h w", w=W)
                for i, (dy, dx) in enumerate(on_pe):
                    (h0, h1), (w0, w1) = span(dy, H), span(dx, W)
                    h0, h1 = max(h0, r * ROWS), min(h1, (r + 1) * ROWS)
                    done = nc.tensor.matmul(sums[:, h0 - r * ROWS:h1 - r * ROWS, w0:w1], diag[:, i, :],
                                            image[:, h0 + dy:h1 + dy, w0 + dx:w1 + dx],
                                            start=i == 0, stop=i == len(on_pe) - 1)
                done.then_inc(part_done, 1)

            def body1(it, last):
                for m in range(IMAGES):
                    n = IMAGES * it + m
                    for b in range(BLOCKS0):
                        if isinstance(n, int) and n == 0 and b:
                            pe.wait_ge(stack_cleared, b)
                        pe.wait_ge(stack_in[b], 48 * (n + 1))
                        for s_ in range(2):
                            stacked(n, b, s_)
                        if b == group1_after(m, last):
                            pe.wait_ge(x1_in[m], 16 * (it + 1))
                            for r in range(PARTS):
                                diagonal(n, m, r, pe_taps(m, last))
            staged(pe, ITS1, body1)

            def project(c, j):
                pe.wait_ge(y_low, c + 1)
                wait(pe, logits_ready, c)
                passes = [(w, y, k) for k in range(G) for w, y in ((proj_for_high, yh), (proj_for_low, yl))]
                for i, (w, y, k) in enumerate(passes):
                    done = nc.tensor.matmul(q_ps[:, :], w[:, k, :], y[:, j % SLOTS, k, :],
                                            start=i == 0, stop=i == len(passes) - 1)
                done.then_inc(q_done, 1)

            def distances(c, j):
                pe.wait_ge(qq_ready, c + 1)
                pixels = qq[:, j % 2, :].rearrange("p (t a i) -> p a t i", t=TILES, i=32)
                for a in range(4):
                    done = nc.tensor.matmul(q_ps[32 * a:32 * a + 32, 0:P], to_dist[:, :], pixels[:, a],
                                            start=True, stop=True)
                done.then_inc(dist_done, 1)

            def experts(c, j, t, halves=(0, 1)):
                for half in halves:
                    if half == 0:
                        wait(pe, expert_added, (E - 2) * (TILES * c + t - 2) + 1)
                    else:
                        wait(pe, mixed, TILES * c + t - 1)
                    passes = [(y, w, k) for k in range(G) for y, w in ((yh, wh), (yh, wl), (yl, wh))]
                    for i, (y, w, k) in enumerate(passes):
                        done = nc.tensor.matmul(expert_ps[t % 2][half][:, :], y[:, j, k, t * P:(t + 1) * P],
                                                w[:, k, half * BANK:(half + 1) * BANK],
                                                start=i == 0, stop=i == len(passes) - 1)
                    done.then_inc(experts_done, 1)

            pe.wait_ge(norm_ready, 1)
            project(0, 0)
            distances(0, 0)

            def body2(it, last):
                for j in range(SLOTS):
                    c = SLOTS * it + j
                    more = not (last and j + 1 >= SLOTS)
                    experts(c, j, 0)
                    if more:
                        project(c + 1, j + 1)
                    experts(c, j, 1)
                    experts(c, j, 2, (0,))
                    if more:
                        distances(c + 1, j + 1)
                    experts(c, j, 2, (1,))
                    experts(c, j, 3)
            staged(pe, ITS2, body2)

        @block.vector
        def _(dve):
            steps = [0]

            def then(instruction):
                instruction.then_inc(setup, 1)
                steps[0] += 1
                dve.wait_ge(setup, steps[0])

            nc.vector.memset(pro[:, :], 0.0)
            then(nc.vector.memset(to_dist[:, :], 0.0))
            nc.vector.memset(to_dist[D:P, 0:E], 1.0).then_inc(cleared, 1)
            nc.vector.memset(stack[0:32, :, 0:W], 0.0)
            nc.vector.memset(stack[64:96, :, HW - W:HW], 0.0)
            nc.vector.memset(stack[96:128, 0, :], 0.0).then_inc(edges_cleared, 1)
            then(nc.vector.memset(stack_w[:, :, :, :], 0.0))
            dve.wait_ge(ident_ready, 1)
            dve.wait_ge(taps_in, 16 * N_TAP_DMAS)
            for d in range(3):
                own = slice(32 * d, 32 * d + 32)
                for b in range(BLOCKS0):
                    for dx in range(3):
                        nc.vector.tensor_scalar(stack_w[own, b, dx, :], ident[own, own],
                                                stack_taps[own, b, dx:dx + 1], None, ALU.mult)
            for i, (dy, dx) in enumerate(LAST_PE_TAPS):
                done = nc.vector.tensor_scalar(diag[:, i, :], ident[:, :], taps[:, tap(dy, dx):tap(dy, dx) + 1],
                                               None, ALU.mult)
            done.then_inc(taps_ready, 1)

            dve.wait_ge(params, 16 * N_PARAM_DMAS)
            for whole, high, low in ((wload, wh[:, :, :], wl[:, :, :]),
                                     (pload[:, :, 0:D], proj_for_high[:, :, 0:D], proj_for_high[:, :, D:2 * D])):
                then(nc.vector.tensor_copy(high, whole))
                nc.vector.tensor_tensor(low, whole, high.bitcast(fp32), ALU.subtract)
            nc.vector.memset(proj_for_low[:, :, 0:D].bitcast(fp32), 0.0)
            nc.vector.tensor_copy(proj_for_low[:, :, D:2 * D], pload[:, :, 0:D])
            nc.vector.memset(st0[:, :, :, :, 0], float(QUARTER))
            nc.vector.memset(st1[:, :, :, 0], float(HW))
            nc.vector.tensor_scalar(to_dist[0:D, 0:E], to_dist[0:D, 0:E], -2.0, None, ALU.mult)
            then(nc.vector.tensor_scalar(gam[:, 1:2], gam[:, 0:1], -1.0, None, ALU.mult))
            then(nc.vector.tensor_tensor(gam[:, 2:3], gam[:, 0:1], gam[:, 1:2], ALU.min))
            dve.wait_ge(norms_ready, 1)
            nc.vector.tensor_tensor(pn2[:, 1:2], pn2[:, 0:1], gam[:, 2:3], ALU.mult).then_inc(weights_ready, 1)

            def body1(it, last):
                between = [len(dve_taps(m, False)) - 1 for m in range(IMAGES)]
                for m in range(IMAGES):
                    n = IMAGES * it + m
                    dve.wait_ge(part_copied, PARTS * (n + 1))
                    image = x1[:, m, :].rearrange("p (h w) -> p h w", w=W)
                    sums = conv1[:, m, :].rearrange("p (h w) -> p h w", w=W)
                    own_taps = dve_taps(m, last)
                    for i, (dy, dx) in enumerate(own_taps):
                        if last and m == IMAGES - 1 and i == len(own_taps) - 1:
                            keep_blocks(n, it, m)
                            dve.wait_ge(blocks_kept, N)
                            combine_blocks(lambda b: st0[:, :, :, b, :].rearrange("p i m s -> p (i m) s"),
                                           BLOCKS0, N * QUARTER)
                        if i:
                            dve.wait_ge(tap_added, sum(between) * it + sum(between[:m]) + i)
                        (h0, h1), (w0, w1) = span(dy, H), span(dx, W)
                        onto = sums[:, h0:h1, w0:w1]
                        done = nc.vector.scalar_tensor_tensor(
                            out=onto, in0=image[:, h0 + dy:h1 + dy, w0 + dx:w1 + dx],
                            scalar=taps[:, tap(dy, dx):tap(dy, dx) + 1], in1=onto, op0=ALU.mult, op1=ALU.add)
                        done.then_inc(tap_added if i < len(own_taps) - 1 else conv_ready, 1)
                    if not (last and m == IMAGES - 1):
                        keep_blocks(n, it, m)
                    if exists(n - IMAGES):
                        keep_image(n - IMAGES, it - 1, m)

            def keep_blocks(n, it, m):
                dve.wait_ge(block_squared, BLOCKS0 * (n + 1))
                nc.vector.tensor_scalar(st0[:, it, m, :, 1], block_minus_mean[:, m, :], -1.0, None, ALU.mult)
                nc.vector.tensor_copy(st0[:, it, m, :, 2], block_squares[:, m, :]).then_inc(blocks_kept, 1)

            def keep_image(n, it, m):
                dve.wait_ge(junk_written, 4 * (n + 1))
                nc.vector.tensor_scalar(st1[:, it, m, 1:2], minus_mean[:, m:m + 1], -1.0, None, ALU.mult)
                nc.vector.tensor_tensor(st1[:, it, m, 2:3], halves[:, m, 1, 0:1], halves[:, m, 1, 1:2],
                                        ALU.add).then_inc(stats1_kept, 1)
            norm_steps = [0]

            def step(instruction):
                instruction.then_inc(norm_step, 1)
                norm_steps[0] += 1
                dve.wait_ge(norm_step, norm_steps[0])

            def normalise(n):
                nc.vector.tensor_scalar(var_eps[:, :], mv[:, :, 1], EPS, None, ALU.add).then_inc(var_ready, 1)
                dve.wait_ge(root_ready, n + 1)
                step(nc.vector.reciprocal(inverse[:, :], root_of[:, :]))
                step(nc.vector.tensor_tensor(newton[:, :], inverse[:, :], inverse[:, :], ALU.mult))
                step(nc.vector.tensor_tensor(newton[:, :], newton[:, :], var_eps[:, :], ALU.mult))
                step(nc.vector.tensor_scalar(newton[:, :], newton[:, :], -0.5, 1.5, ALU.mult, ALU.add))
                step(nc.vector.tensor_tensor(inverse[:, :], inverse[:, :], newton[:, :], ALU.mult))
                step(nc.vector.tensor_tensor(aff[:, n, 0], inverse[:, :], bnp[:, 2 * n], ALU.mult))
                step(nc.vector.tensor_tensor(newton[:, :], mv[:, :, 0], aff[:, n, 0], ALU.mult))
                nc.vector.tensor_tensor(aff[:, n, 1], bnp[:, 2 * n + 1], newton[:, :],
                                        ALU.subtract).then_inc(norm_ready, 1)
            def combine_blocks(stats, blocks, count):
                for b in range(blocks):
                    done = nc.vector.bn_aggr(block_mv[:, b, :], stats(b))
                step(done)
                nc.vector.memset(block_st[:, 0:blocks, 0], float(count))
                nc.vector.tensor_copy(block_st[:, 0:blocks, 1], block_mv[:, 0:blocks, 0])
                nc.vector.tensor_scalar(block_st[:, 0:blocks, 2], block_mv[:, 0:blocks, 1], float(count), None,
                                        ALU.mult).then_inc(blocks_ready, 1)

            staged(dve, ITS1, body1)
            dve.wait_ge(conv_ready, N)
            for r in range(PARTS):
                at = N - 1 + 2 * r
                done = nc.vector.bn_stats(st1_flat[:, at:at + 2, :].rearrange("p i s -> p (i s)"),
                                          conv1[:, IMAGES - 1, r * ROWS * W:(r + 1) * ROWS * W])
            done.then_inc(last_measured, 1)
            keep_image(N - 2, ITS1 - 1, 0)
            dve.wait_ge(last_measured, 1)
            dve.wait_ge(stats1_kept, N - 1)
            step(nc.vector.bn_aggr(mv[:, 1, :], st1_flat[:, 0:N - 1 + 2 * PARTS, :]))
            dve.wait_ge(blocks_in, 16 * BLOCKS0)
            step(nc.vector.bn_aggr(mv[:, 0, :], channel_st[:, 0]))
            normalise(0)

            def sum_q(c, j):
                dve.wait_ge(cross_ready, c + 1)
                wait(dve, dist_done, c - 1)
                nc.vector.tensor_tensor(qq[0:D, j % 2], q_ps[0:D, :], q_cross[:, :], ALU.add).then_inc(q_ready, 1)

            def turn(c, j):
                dve.wait_ge(logits_ready, c + 1)
                wait(dve, centered_ready, c)
                nc.vector.transpose(logit_t[:, :, :].rearrange("p t e -> p (t e)"),
                                    logit_rows[:, j % 2]).then_inc(turned, 1)

            def find_top(c, j):
                dve.wait_ge(turned, c + 1)
                nc.vector.tensor_reduce(out=top[:, :], in_=logit_t[:, :, 0:E], axis=AX.X,
                                        op=ALU.max).then_inc(top_ready, 1)

            def center(c, j):
                dve.wait_ge(top_ready, c + 1)
                nc.vector.tensor_tensor(centered[:, j % 2], logit_t[:, :, 0:E],
                                        top[:, :].unsqueeze(2).broadcast_to([P, TILES, E]),
                                        ALU.subtract).then_inc(centered_ready, 1)

            def sum_exps(c, j):
                dve.wait_ge(exp_ready, c + 1)
                wait(dve, gates_ready, c)
                nc.vector.tensor_reduce(out=total[:, :], in_=ex[:, j % 2], axis=AX.X,
                                        op=ALU.add).then_inc(total_ready, 1)

            def invert(c, j):
                dve.wait_ge(total_ready, c + 1)
                nc.vector.reciprocal(inv_total[:, :], total[:, :]).then_inc(inverse_ready, 1)

            def gates(c, j):
                dve.wait_ge(inverse_ready, c + 1)
                wait(dve, mixed, TILES * (c - 1))
                nc.vector.tensor_tensor(gate[:, j % 2], ex[:, j % 2],
                                        inv_total[:, :].unsqueeze(2).broadcast_to([P, TILES, E]),
                                        ALU.mult).then_inc(gates_ready, 1)

            def add_expert(c, j, t, e):
                if e == 1:
                    dve.wait_ge(mix_begun, TILES * c + t + 1)
                else:
                    dve.wait_ge(expert_added, (E - 2) * (TILES * c + t) + e - 1)
                if e == 2:
                    dve.wait_ge(experts_done, 2 * (TILES * c + t + 1))
                nc.vector.scalar_tensor_tensor(
                    out=mix[:, t], in0=expert_ps[t % 2][e // 2][:, (e % 2) * COUT:(e % 2 + 1) * COUT],
                    scalar=gate[:, j % 2, t, e:e + 1], in1=mix[:, t],
                    op0=ALU.mult, op1=ALU.add).then_inc(expert_added if e < E - 1 else mixed, 1)

            def transpose(c, it, j, t):
                dve.wait_ge(mixed, TILES * c + t + 1)
                if t == 0:
                    wait(dve, mix_out[j], 64 * it)
                    if j % 2 == 0:
                        wait(dve, mix_measured, c - 2)
                nc.vector.transpose(mo[:, j // 2, :, j % 2, t * 32:(t + 1) * 32],
                                    mix[:, t].rearrange("p (b q) -> p b q", q=32)).then_inc(transposed, 1)

            def measure(c, it, j, t):
                if j == 2 and t == 0:
                    wait(dve, stats2_kept, it)
                if t == 0:
                    dve.wait_ge(transposed, TILES * (c - j % 2))
                pair, b = 1 - j // 2, 4 * (j % 2) + t
                done = nc.vector.bn_stats(st2[:, pair, b, :], mo[:, pair, b].rearrange("p r q -> p (r q)"))
                if t == TILES - 1:
                    done.then_inc(mix_measured, 1)

            def aggregate(it):
                dve.wait_ge(mix_measured, SLOTS * (it + 1))
                nc.vector.tensor_scalar(st2_all[:, it, :, 0], st2[:, 0, :, 0], float(SLOTS), None, ALU.mult)
                for b in range(BLOCKS):
                    done = nc.vector.bn_aggr(body_mv[:, b, :], st2[:, :, b, :])
                done.then_inc(body_aggregated, 1)
                dve.wait_ge(body_aggregated, it + 1)
                nc.vector.tensor_copy(st2_all[:, it, :, 1], body_mv[:, :, 0])
                nc.vector.tensor_scalar(st2_all[:, it, :, 2], body_mv[:, :, 1], float(SLOTS * P), None,
                                        ALU.mult).then_inc(stats2_kept, 1)

            sum_q(0, 0)
            for step_of_softmax in (turn, find_top, center, sum_exps, invert, gates):
                step_of_softmax(0, 0)

            def body2(it, last):
                for j in range(SLOTS):
                    c = SLOTS * it + j
                    more = not (last and j + 1 >= SLOTS)
                    soon = [[], [], [turn, find_top, center], [sum_exps, invert, gates]]
                    for t in range(TILES):
                        steps = soon[t] if more else []
                        for e in range(1, E):
                            add_expert(c, j, t, e)
                            if steps:
                                steps[e - 1](c + 1, j + 1)
                            if e == 1 and t:
                                transpose(c, it, j, t - 1)
                            elif e == 1 and exists(c - 1):
                                transpose(c - 1, it if j else it - 1, (j - 1) % SLOTS, TILES - 1)
                            if e == 2 and exists(c - 2):
                                measure(c, it, j, t)
                        if t == 0 and more:
                            sum_q(c + 1, j + 1)
                    if j == 1 and exists(it - 1):
                        aggregate(it - 1)
            staged(dve, ITS2, body2)
            transpose(CHUNKS - 1, ITS2 - 1, SLOTS - 1, TILES - 1)
            for j in range(2):
                for t in range(TILES):
                    measure(CHUNKS + j, ITS2, j, t)
            aggregate(ITS2 - 1)
            dve.wait_ge(stats2_kept, ITS2)
            combine_blocks(lambda b: st2_all[:, :, b, :], BLOCKS, CHUNKS * 32 * TILES)
            dve.wait_ge(blocks_in, 16 * (BLOCKS0 + BLOCKS))
            for g in range(G):
                step(nc.vector.bn_aggr(mv[:, g, :], channel_st[:, g]))
            normalise(1)

            def body3(it, last):
                for k in slots_of(last):
                    dve.wait_ge(*((last_x_in, 16) if k == LAST else (x_again[k], 16 * (it + 1))))
                    dve.wait_ge(*((last_mix_in, 16) if k == LAST else (mix_in[k], 16 * (it + 1))))
                    mixture, x_of = (last_mix, last_x[:, :]) if k == LAST else (xb[:, k, :], yb[:, k, :])
                    nc.vector.scalar_tensor_tensor(out=mixture, in0=mixture,
                                                   scalar=aff[:, 1, 0, k % G:k % G + 1], in1=x_of,
                                                   op0=ALU.mult, op1=ALU.add).then_inc(summed, 1)
            staged(dve, ITS3, body3)


def kernel(**inputs):
    import numpy as np
    import concourse.bacc as bacc
    from concourse.bass_utils import run_bass_kernel_spmd

    arr = {k.replace("L0_conv_", ""): np.asarray(v) for k, v in inputs.items()}
    laid = {
        "x": arr["x"],
        "dw": arr["dw_w"].reshape(C, 9),
        "bn1s": arr["bn1_scale"], "bn1b": arr["bn1_bias"],
        "projT": arr["proj_w"].T, "projb": arr["proj_b"],
        "proto": arr["prototypes"], "protoT": arr["prototypes"].T,
        "gamma": arr["gamma"].reshape(1),
        "expT": arr["expert_w"].transpose(2, 0, 1).reshape(C, E * COUT),
        "bn2s": arr["bn2_scale"], "bn2b": arr["bn2_bias"],
    }
    laid = {k: np.ascontiguousarray(v) for k, v in laid.items()}
    nc = bacc.Bacc("TRN2", target_bir_lowering=False, num_devices=1)
    args = [nc.dram_tensor(f"in_{k}", v.shape, mybir.dt.from_np(v.dtype), kind="ExternalInput").ap() for k, v in laid.items()]
    out = nc.dram_tensor("out", (N, COUT, H, W), fp32, kind="ExternalOutput").ap()
    build(nc, *args, out)
    result = run_bass_kernel_spmd(nc, [{f"in_{k}": v for k, v in laid.items()}], core_ids=[0])
    return result.results[0]["out"]
```
